# Optimizing a Trainium2 kernel written in Bass

```python
import numpy as np
import jax
import jax.numpy as jnp

def _softmax(x, axis=-1):
    return jax.nn.softmax(x, axis=axis)

def _gelu(x):
    return jax.nn.gelu(x, approximate=True)

def _silu(x):
    return jax.nn.silu(x)

def _sigmoid(x):
    return jax.nn.sigmoid(x)

def _layernorm(x, axis=-1, eps=1e-05):
    m = jnp.mean(x, axis=axis, keepdims=True)
    v = jnp.var(x, axis=axis, keepdims=True)
    return (x - m) / jnp.sqrt(v + eps)

def _scatter_add(tgt, idx, src, axis=0):
    return tgt.at[idx].add(src)

def _segment_sum(src, seg, n):
    return jax.ops.segment_sum(src, seg, n)
kernel_name = 'mk_xattn_ffn_d4_seqx_r4_1d71c7'

def setup_inputs(seed: int=0):
    np.random.seed(seed)
    _w = jnp.asarray

    def _rec_inputs():
        import jax
        import jax.numpy as jnp
        _rk = jax.random.key(seed)
        x = -0.0003929 + 0.9999 * jax.random.normal(jax.random.fold_in(_rk, 1), (8, 256, 256), jnp.float32)
        _lenS = 256 - jax.random.randint(jax.random.fold_in(_rk, 7), (8,), 0, max(1, 256 // 4) + 1, jnp.int32)
        _lenS2 = 120 - jax.random.randint(jax.random.fold_in(_rk, 8), (8,), 0, max(1, 120 // 4) + 1, jnp.int32)
        _ctx_1024P = jax.random.normal(jax.random.fold_in(_rk, 11), (8, 16, 256), jnp.float32)
        _ctx_1024c = jax.random.dirichlet(jax.random.fold_in(_rk, 511), 0.3 * jnp.ones((16,), jnp.float32), (8, 120))
        _ctx_1024t = jnp.einsum('bsk,bkd->bsd', _ctx_1024c, _ctx_1024P)
        _ctx_1024t = _ctx_1024t * jax.lax.rsqrt(jnp.mean(jnp.square(_ctx_1024t)) + 1e-12) * 0.953939
        ctx_1024 = 2.81802e-05 + 1.00001 * (_ctx_1024t + 0.3 * jax.random.normal(jax.random.fold_in(_rk, 611), (8, 120, 256), jnp.float32))
        _validS = jnp.arange(256)[None, :] < _lenS[:, None]
        _validS2 = jnp.arange(120)[None, :] < _lenS2[:, None]
        _causal = jnp.tril(jnp.ones((256, 256), dtype=bool))
        mask_BxS2x1_ff1 = jnp.where(jnp.ones((8, 120, 1), dtype=bool), 1.0, 0.0).astype(jnp.float32)
        mask_Bx1xSxS2_ik1 = jnp.where(jnp.broadcast_to(_validS2[:, None, None, :], (8, 1, 256, 120)), 1, 0).astype(jnp.int32)
        mask_BxS2_bk0 = jnp.logical_not(jnp.broadcast_to(_validS2[:, :], (8, 120)))
        mask_SxS2_bk1 = jnp.broadcast_to(_validS2[0:1, :], (256, 120))
        return (x, ctx_1024, mask_BxS2x1_ff1, mask_Bx1xSxS2_ik1, mask_BxS2_bk0, mask_SxS2_bk1)
    x, ctx_1024, mask_BxS2x1_ff1, mask_Bx1xSxS2_ik1, mask_BxS2_bk0, mask_SxS2_bk1 = _rec_inputs()

    def _L0_xattn_setup():
        import jax, jax.numpy as jnp
        import numpy as np
        B, S, U = (4, 1024, 256)
        key = jax.random.key(seed)
        ks = jax.random.split(key, 8)
        scale = 1.0 / np.sqrt(U)
        return {'query': jax.random.normal(ks[0], (B, S, U), dtype=jnp.float32), 'key': jax.random.normal(ks[1], (B, S, U), dtype=jnp.float32), 'value': jax.random.normal(ks[2], (B, S, U), dtype=jnp.float32), 'mask': jnp.ones((B, S, 1), dtype=jnp.float32), 'Wk': jax.random.normal(ks[3], (U, U), dtype=jnp.float32) * scale, 'Wv': jax.random.normal(ks[4], (U, U), dtype=jnp.float32) * scale, 'Wq': jax.random.normal(ks[5], (U, U), dtype=jnp.float32) * scale, 'Wo': jax.random.normal(ks[6], (U, U), dtype=jnp.float32) * scale}
    _L0_xattn_all = _L0_xattn_setup()
    _L0_xattn_in = {k: v for k, v in _L0_xattn_all.items() if k in ('Wk', 'Wv', 'Wq', 'Wo')}
    del _L0_xattn_all

    def _L0_ffn_setup():
        import jax, jax.numpy as jnp
        import numpy as np
        DIM = 256
        DEPTH = 7
        PAR = 8
        N_NODES = 2 ** (DEPTH + 1) - 1
        WIDTH = PAR * N_NODES
        key = jax.random.key(seed)
        k1, k2, k3, k4 = jax.random.split(key, 4)
        init_k = float(np.sqrt(1.0 / DIM))
        init_k2 = float(np.sqrt(1.0 / ((DEPTH + 1) * PAR)))
        oldx = jax.random.normal(k1, (4, 512, DIM), dtype=jnp.float32)
        W_in = jax.random.uniform(k2, (WIDTH, DIM), jnp.float32, -init_k, init_k)
        b_in = jax.random.uniform(k3, (WIDTH,), jnp.float32, -init_k, init_k)
        W_out = jax.random.uniform(k4, (DIM, WIDTH), jnp.float32, -init_k2, init_k2)
        return {'oldx': oldx, 'W_in': W_in, 'b_in': b_in, 'W_out': W_out}
    _L0_ffn_all = _L0_ffn_setup()
    _L0_ffn_in = {k: v for k, v in _L0_ffn_all.items() if k in ('W_in', 'b_in', 'W_out')}
    del _L0_ffn_all

    def _L1_xattn_setup():
        import jax, jax.numpy as jnp
        import numpy as np
        EMBED = 256
        HEADS = 16
        HEAD_DIM = EMBED // HEADS
        key = jax.random.key(seed)
        ks = jax.random.split(key, 7)
        N, L = (2, 512)
        values = jax.random.normal(ks[0], (N, L, EMBED), dtype=jnp.float32)
        keys = jax.random.normal(ks[1], (N, L, EMBED), dtype=jnp.float32)
        queries = jax.random.normal(ks[2], (N, L, EMBED), dtype=jnp.float32)
        mask = jax.random.randint(ks[3], (N, 1, L, L), 0, 2, dtype=jnp.int32)
        s = 1.0 / np.sqrt(HEAD_DIM)
        Wv = jax.random.normal(ks[4], (HEAD_DIM, HEAD_DIM), dtype=jnp.float32) * s
        Wk = jax.random.normal(ks[5], (HEAD_DIM, HEAD_DIM), dtype=jnp.float32) * s
        Wq = jax.random.normal(ks[6], (HEAD_DIM, HEAD_DIM), dtype=jnp.float32) * s
        return {'values': values, 'keys': keys, 'queries': queries, 'mask': mask, 'Wv': Wv, 'Wk': Wk, 'Wq': Wq}
    _L1_xattn_all = _L1_xattn_setup()
    _L1_xattn_in = {k: v for k, v in _L1_xattn_all.items() if k in ('Wv', 'Wk', 'Wq')}
    del _L1_xattn_all

    def _L1_ffn_setup():
        import jax, jax.numpy as jnp
        import numpy as np
        B, S, D_MODEL, D_HIDDEN = (4, 512, 256, 1024)

        def act_quant(x):
            scale = 127.0 / jnp.clip(jnp.max(jnp.abs(x), axis=-1, keepdims=True), 1e-05)
            return jnp.clip(jnp.round(x * scale), -128, 127) / scale

        def weight_quant(w):
            scale = 1.0 / jnp.clip(jnp.mean(jnp.abs(w)), 1e-05)
            return jnp.clip(jnp.round(w * scale), -1, 1) / scale

        def bit_linear(x, w):
            xq = x + jax.lax.stop_gradient(act_quant(x) - x)
            wq = w + jax.lax.stop_gradient(weight_quant(w) - w)
            return jnp.einsum('bsd,hd->bsh', xq, wq)

        def depthwise_conv1d(x_bcl, w, b):
            y = jax.lax.conv_general_dilated(x_bcl, w, window_strides=(1,), padding=[(1, 1)], dimension_numbers=('NCH', 'OIH', 'NCH'), feature_group_count=x_bcl.shape[1])
            return y + b[None, :, None]
        key = jax.random.key(seed)
        ks = jax.random.split(key, 5)
        lim1 = 1.0 / np.sqrt(D_MODEL)
        lim2 = 1.0 / np.sqrt(D_HIDDEN)
        limc = 1.0 / np.sqrt(3.0)
        return {'x': jax.random.normal(ks[0], (B, S, D_MODEL), dtype=jnp.float32), 'w1': jax.random.uniform(ks[1], (D_HIDDEN, D_MODEL), jnp.float32, -lim1, lim1), 'conv_w': jax.random.uniform(ks[2], (D_HIDDEN, 1, 3), jnp.float32, -limc, limc), 'conv_b': jax.random.uniform(ks[3], (D_HIDDEN,), jnp.float32, -limc, limc), 'w2': jax.random.uniform(ks[4], (D_MODEL, D_HIDDEN), jnp.float32, -lim2, lim2)}
    _L1_ffn_all = _L1_ffn_setup()
    _L1_ffn_in = {k: v for k, v in _L1_ffn_all.items() if k in ('w1', 'conv_w', 'conv_b', 'w2')}
    del _L1_ffn_all

    def _L2_xattn_setup():
        import jax, jax.numpy as jnp
        import numpy as np
        N_HEAD = 16
        D_MODEL = 256
        HEAD_DIM = D_MODEL // N_HEAD

        def _split_heads(x):
            B, S, D = x.shape
            return x.reshape(B, S, N_HEAD, HEAD_DIM).transpose(0, 2, 1, 3)
        key = jax.random.key(seed)
        ks = jax.random.split(key, 12)
        B, S, D = (2, 512, D_MODEL)
        scale = 1.0 / np.sqrt(D)
        inp = {'q': jax.random.normal(ks[0], (B, S, D), jnp.float32), 'k': jax.random.normal(ks[1], (B, S, D), jnp.float32), 'v': jax.random.normal(ks[2], (B, S, D), jnp.float32), 'mask': jax.random.randint(ks[3], (B, 1, S, S), 0, 2, jnp.int32), 'wq': jax.random.normal(ks[4], (D, D), jnp.float32) * scale, 'bq': jnp.zeros((D,), jnp.float32), 'wk': jax.random.normal(ks[5], (D, D), jnp.float32) * scale, 'bk': jnp.zeros((D,), jnp.float32), 'wv': jax.random.normal(ks[6], (D, D), jnp.float32) * scale, 'bv': jnp.zeros((D,), jnp.float32), 'wo': jax.random.normal(ks[7], (D, D), jnp.float32) * scale, 'bo': jnp.zeros((D,), jnp.float32)}
        return inp
    _L2_xattn_all = _L2_xattn_setup()
    _L2_xattn_in = {k: v for k, v in _L2_xattn_all.items() if k in ('wq', 'bq', 'wk', 'bk', 'wv', 'bv', 'wo', 'bo')}
    del _L2_xattn_all

    def _L2_ffn_setup():
        import jax, jax.numpy as jnp
        import numpy as np
        D_IN, D_HID = (256, 1024)

        def _ternary(key, shape):
            return jax.random.randint(key, shape, -1, 2).astype(jnp.float32)

        def _tlin(x, w, s):
            return jnp.einsum('bsi,oi->bso', x, w) * s
        key = jax.random.key(seed)
        ks = jax.random.split(key, 12)
        inv = lambda fan: 1.0 / np.sqrt(fan).astype(np.float32)
        return {'x': jax.random.normal(ks[0], (4, 512, D_IN), dtype=jnp.float32), 'w1_w': _ternary(ks[1], (D_HID, D_IN)), 'w1_s': jax.random.uniform(ks[2], (D_HID,), dtype=jnp.float32) * inv(D_IN), 'w2_w': _ternary(ks[3], (D_HID, D_IN)), 'w2_s': jax.random.uniform(ks[4], (D_HID,), dtype=jnp.float32) * inv(D_IN), 'h1_w': _ternary(ks[5], (D_HID, D_HID)), 'h1_s': jax.random.uniform(ks[6], (D_HID,), dtype=jnp.float32) * inv(D_HID), 'h2_w': _ternary(ks[7], (D_HID, D_HID)), 'h2_s': jax.random.uniform(ks[8], (D_HID,), dtype=jnp.float32) * inv(D_HID), 'w3_w': _ternary(ks[9], (D_IN, D_HID)), 'w3_s': jax.random.uniform(ks[10], (D_IN,), dtype=jnp.float32) * inv(D_HID)}
    _L2_ffn_all = _L2_ffn_setup()
    _L2_ffn_in = {k: v for k, v in _L2_ffn_all.items() if k in ('w1_w', 'w1_s', 'w2_w', 'w2_s', 'h1_w', 'h1_s', 'h2_w', 'h2_s', 'w3_w', 'w3_s')}
    del _L2_ffn_all

    def _L3_xattn_setup():
        import jax, jax.numpy as jnp
        import numpy as np
        B, T, D, H = (2, 512, 256, 32)
        NEG = -1000000000.0
        key = jax.random.key(seed)
        ks = jax.random.split(key, 8)
        q = jax.random.normal(ks[0], (B, T, D), jnp.float32)
        k = jax.random.normal(ks[1], (B, T, D), jnp.float32)
        v = jax.random.normal(ks[2], (B, T, D), jnp.float32)
        Wqkv = jax.random.normal(ks[3], (D, 3 * D), jnp.float32) * 0.02
        bqkv = jax.random.normal(ks[4], (3 * D,), jnp.float32) * 0.02
        Wo = jax.random.normal(ks[5], (D, D), jnp.float32) * 0.02
        bo = jax.random.normal(ks[6], (D,), jnp.float32) * 0.02
        key_padding_mask = jnp.zeros((B, T), bool).at[1, T - 128:].set(True)
        attn_mask = jnp.triu(jnp.ones((T, T), bool), k=1)
        return {'q': q, 'k': k, 'v': v, 'Wqkv': Wqkv, 'bqkv': bqkv, 'Wo': Wo, 'bo': bo, 'key_padding_mask': key_padding_mask, 'attn_mask': attn_mask, 'n_heads': H}
    _L3_xattn_all = _L3_xattn_setup()
    _L3_xattn_in = {k: v for k, v in _L3_xattn_all.items() if k in ('Wqkv', 'bqkv', 'Wo', 'bo')}
    del _L3_xattn_all

    def _L3_ffn_setup():
        import jax, jax.numpy as jnp
        import numpy as np
        D = 256
        E = 8
        key = jax.random.key(seed)
        ks = jax.random.split(key, 7)
        s = 1.0 / np.sqrt(D)
        x = jax.random.normal(ks[0], (4, 512, D), dtype=jnp.float32)
        Wg = jax.random.uniform(ks[1], (D, E), minval=-s, maxval=s, dtype=jnp.float32)
        bg = jax.random.uniform(ks[2], (E,), minval=-s, maxval=s, dtype=jnp.float32)
        W1 = jax.random.uniform(ks[3], (E, D, D), minval=-s, maxval=s, dtype=jnp.float32)
        b1 = jax.random.uniform(ks[4], (E, D), minval=-s, maxval=s, dtype=jnp.float32)
        W2 = jax.random.uniform(ks[5], (E, D, D), minval=-s, maxval=s, dtype=jnp.float32)
        b2 = jax.random.uniform(ks[6], (E, D), minval=-s, maxval=s, dtype=jnp.float32)
        return {'x': x, 'Wg': Wg, 'bg': bg, 'W1': W1, 'b1': b1, 'W2': W2, 'b2': b2}
    _L3_ffn_all = _L3_ffn_setup()
    _L3_ffn_in = {k: v for k, v in _L3_ffn_all.items() if k in ('Wg', 'bg', 'W1', 'b1', 'W2', 'b2')}
    del _L3_ffn_all
    return {'x': x, 'ctx_1024': ctx_1024, 'mask_BxS2x1_ff1': mask_BxS2x1_ff1, 'mask_Bx1xSxS2_ik1': mask_Bx1xSxS2_ik1, 'mask_BxS2_bk0': mask_BxS2_bk0, 'mask_SxS2_bk1': mask_SxS2_bk1, 'L0_xattn_Wk': _L0_xattn_in['Wk'], 'L0_xattn_Wv': _L0_xattn_in['Wv'], 'L0_xattn_Wq': _L0_xattn_in['Wq'], 'L0_xattn_Wo': _L0_xattn_in['Wo'], 'L0_ffn_W_in': _L0_ffn_in['W_in'], 'L0_ffn_b_in': _L0_ffn_in['b_in'], 'L0_ffn_W_out': _L0_ffn_in['W_out'], 'L1_xattn_Wv': _L1_xattn_in['Wv'], 'L1_xattn_Wk': _L1_xattn_in['Wk'], 'L1_xattn_Wq': _L1_xattn_in['Wq'], 'L1_ffn_w1': _L1_ffn_in['w1'], 'L1_ffn_conv_w': _L1_ffn_in['conv_w'], 'L1_ffn_conv_b': _L1_ffn_in['conv_b'], 'L1_ffn_w2': _L1_ffn_in['w2'], 'L2_xattn_wq': _L2_xattn_in['wq'], 'L2_xattn_bq': _L2_xattn_in['bq'], 'L2_xattn_wk': _L2_xattn_in['wk'], 'L2_xattn_bk': _L2_xattn_in['bk'], 'L2_xattn_wv': _L2_xattn_in['wv'], 'L2_xattn_bv': _L2_xattn_in['bv'], 'L2_xattn_wo': _L2_xattn_in['wo'], 'L2_xattn_bo': _L2_xattn_in['bo'], 'L2_ffn_w1_w': _L2_ffn_in['w1_w'], 'L2_ffn_w1_s': _L2_ffn_in['w1_s'], 'L2_ffn_w2_w': _L2_ffn_in['w2_w'], 'L2_ffn_w2_s': _L2_ffn_in['w2_s'], 'L2_ffn_h1_w': _L2_ffn_in['h1_w'], 'L2_ffn_h1_s': _L2_ffn_in['h1_s'], 'L2_ffn_h2_w': _L2_ffn_in['h2_w'], 'L2_ffn_h2_s': _L2_ffn_in['h2_s'], 'L2_ffn_w3_w': _L2_ffn_in['w3_w'], 'L2_ffn_w3_s': _L2_ffn_in['w3_s'], 'L3_xattn_Wqkv': _L3_xattn_in['Wqkv'], 'L3_xattn_bqkv': _L3_xattn_in['bqkv'], 'L3_xattn_Wo': _L3_xattn_in['Wo'], 'L3_xattn_bo': _L3_xattn_in['bo'], 'L3_ffn_Wg': _L3_ffn_in['Wg'], 'L3_ffn_bg': _L3_ffn_in['bg'], 'L3_ffn_W1': _L3_ffn_in['W1'], 'L3_ffn_b1': _L3_ffn_in['b1'], 'L3_ffn_W2': _L3_ffn_in['W2'], 'L3_ffn_b2': _L3_ffn_in['b2']}

def reference(x, ctx_1024, mask_BxS2x1_ff1, mask_Bx1xSxS2_ik1, mask_BxS2_bk0, mask_SxS2_bk1, L0_xattn_Wk, L0_xattn_Wv, L0_xattn_Wq, L0_xattn_Wo, L0_ffn_W_in, L0_ffn_b_in, L0_ffn_W_out, L1_xattn_Wv, L1_xattn_Wk, L1_xattn_Wq, L1_ffn_w1, L1_ffn_conv_w, L1_ffn_conv_b, L1_ffn_w2, L2_xattn_wq, L2_xattn_bq, L2_xattn_wk, L2_xattn_bk, L2_xattn_wv, L2_xattn_bv, L2_xattn_wo, L2_xattn_bo, L2_ffn_w1_w, L2_ffn_w1_s, L2_ffn_w2_w, L2_ffn_w2_s, L2_ffn_h1_w, L2_ffn_h1_s, L2_ffn_h2_w, L2_ffn_h2_s, L2_ffn_w3_w, L2_ffn_w3_s, L3_xattn_Wqkv, L3_xattn_bqkv, L3_xattn_Wo, L3_xattn_bo, L3_ffn_Wg, L3_ffn_bg, L3_ffn_W1, L3_ffn_b1, L3_ffn_W2, L3_ffn_b2):
    import jax
    import jax.numpy as jnp

    def _L0_xattn_ref(query, key, value, mask, Wk, Wv, Wq, Wo):
        import jax, jax.numpy as jnp
        import numpy as np
        B, S, U = (4, 1024, 256)
        pk = jnp.einsum('bsu,uv->bsv', key, Wk)
        pv = jnp.einsum('bsu,uv->bsv', value, Wv)
        pq = jnp.einsum('bsu,uv->bsv', query, Wq)
        pk = pk * mask
        pv = pv * mask
        pk = jax.nn.swish(pk)
        kv = jnp.einsum('bsu,bsv->buv', pk, pv)
        out = jnp.einsum('bsu,buv->bsv', pq, kv)
        return jnp.einsum('bsu,uv->bsv', out, Wo)

    def _L0_ffn_ref(oldx, W_in, b_in, W_out):
        import jax, jax.numpy as jnp
        import numpy as np
        DIM = 256
        DEPTH = 7
        PAR = 8
        N_NODES = 2 ** (DEPTH + 1) - 1
        WIDTH = PAR * N_NODES
        x = oldx.reshape(-1, DIM)
        B = x.shape[0]
        logits = x @ W_in.T + b_in
        decisions = (logits > 0).astype(jnp.int32).reshape(B, PAR, N_NODES)
        acts = jax.nn.silu(logits).reshape(B, PAR, N_NODES)
        current = jnp.zeros((B, PAR), dtype=jnp.int32)
        dmap = jax.nn.one_hot(current, N_NODES, dtype=acts.dtype)
        for d in range(DEPTH):
            cur_platform = 2 ** d - 1
            next_platform = 2 ** (d + 1) - 1
            moves = jnp.take_along_axis(decisions, current[..., None], axis=2)[..., 0]
            current = (current - cur_platform) * 2 + moves + next_platform
            dmap = dmap + jax.nn.one_hot(current, N_NODES, dtype=acts.dtype)
        masked = acts * jax.lax.stop_gradient(dmap)
        out = masked.reshape(B, WIDTH) @ W_out.T
        return out.reshape(oldx.shape)

    def _L1_xattn_ref(values, keys, queries, mask, Wv, Wk, Wq):
        import jax, jax.numpy as jnp
        import numpy as np
        EMBED = 256
        HEADS = 16
        HEAD_DIM = EMBED // HEADS
        N, Lq = (queries.shape[0], queries.shape[1])
        Lk = keys.shape[1]
        v = values.reshape(N, Lk, HEADS, HEAD_DIM) @ Wv.T
        k = keys.reshape(N, Lk, HEADS, HEAD_DIM) @ Wk.T
        q = queries.reshape(N, Lq, HEADS, HEAD_DIM) @ Wq.T
        e = jnp.einsum('nqhd,nkhd->nhqk', q, k) / jnp.sqrt(jnp.float32(EMBED))
        e = jnp.where(mask == 0, jnp.float32(-1e+20), e)
        attn = jax.nn.softmax(e, axis=-1)
        out = jnp.einsum('nhqk,nkhd->nqhd', attn, v)
        return out.reshape(N, Lq, HEADS * HEAD_DIM)

    def _L1_ffn_ref(x, w1, conv_w, conv_b, w2):
        import jax, jax.numpy as jnp
        import numpy as np
        B, S, D_MODEL, D_HIDDEN = (4, 512, 256, 1024)

        def act_quant(x):
            scale = 127.0 / jnp.clip(jnp.max(jnp.abs(x), axis=-1, keepdims=True), 1e-05)
            return jnp.clip(jnp.round(x * scale), -128, 127) / scale

        def weight_quant(w):
            scale = 1.0 / jnp.clip(jnp.mean(jnp.abs(w)), 1e-05)
            return jnp.clip(jnp.round(w * scale), -1, 1) / scale

        def bit_linear(x, w):
            xq = x + jax.lax.stop_gradient(act_quant(x) - x)
            wq = w + jax.lax.stop_gradient(weight_quant(w) - w)
            return jnp.einsum('bsd,hd->bsh', xq, wq)

        def depthwise_conv1d(x_bcl, w, b):
            y = jax.lax.conv_general_dilated(x_bcl, w, window_strides=(1,), padding=[(1, 1)], dimension_numbers=('NCH', 'OIH', 'NCH'), feature_group_count=x_bcl.shape[1])
            return y + b[None, :, None]
        h = bit_linear(x, w1)
        h = depthwise_conv1d(h.transpose(0, 2, 1), conv_w, conv_b)
        h = h.transpose(0, 2, 1)
        h = jax.nn.silu(h)
        return bit_linear(h, w2)

    def _L2_xattn_ref(q, k, v, mask, wq, bq, wk, bk, wv, bv, wo, bo):
        import jax, jax.numpy as jnp
        import numpy as np
        N_HEAD = 16
        D_MODEL = 256
        HEAD_DIM = D_MODEL // N_HEAD

        def _split_heads(x):
            B, S, D = x.shape
            return x.reshape(B, S, N_HEAD, HEAD_DIM).transpose(0, 2, 1, 3)
        _q = _split_heads(q @ wq + bq)
        _k = _split_heads(k @ wk + bk)
        _v = _split_heads(v @ wv + bv)
        inv = 1.0 / (jnp.sqrt(jnp.float32(HEAD_DIM)) + 1e-08)
        score = jnp.einsum('bhqd,bhkd->bhqk', _q, _k) * inv
        score = score + mask.astype(score.dtype) * -1000000000.0
        attn = jax.nn.softmax(score, axis=-1)
        ctx = jnp.einsum('bhqk,bhkd->bhqd', attn, _v)
        B, H, S, Hd = ctx.shape
        ctx = ctx.transpose(0, 2, 1, 3).reshape(B, S, H * Hd)
        return ctx @ wo + bo

    def _L2_ffn_ref(x, w1_w, w1_s, w2_w, w2_s, h1_w, h1_s, h2_w, h2_s, w3_w, w3_s):
        import jax, jax.numpy as jnp
        import numpy as np
        D_IN, D_HID = (256, 1024)

        def _ternary(key, shape):
            return jax.random.randint(key, shape, -1, 2).astype(jnp.float32)

        def _tlin(x, w, s):
            return jnp.einsum('bsi,oi->bso', x, w) * s
        h = jax.nn.silu(_tlin(x, w1_w, w1_s)) * _tlin(x, w2_w, w2_s)
        h = jax.nn.gelu(_tlin(h, h1_w, h1_s), approximate=False)
        h = jax.nn.gelu(_tlin(h, h2_w, h2_s), approximate=False)
        return _tlin(h, w3_w, w3_s)

    def _L3_xattn_ref(q, k, v, Wqkv, bqkv, Wo, bo, key_padding_mask, attn_mask, n_heads):
        import jax, jax.numpy as jnp
        import numpy as np
        B, T, D, H = (2, 512, 256, 32)
        NEG = -1000000000.0
        Bq, T1, Dm = q.shape
        T2 = k.shape[1]
        dh = Dm // n_heads
        x = jnp.concatenate([q, k, v], axis=1)
        proj = x @ Wqkv + bqkv
        proj = proj.reshape(Bq, -1, 3, n_heads, dh)
        qp = proj[:, :T1, 0]
        kp = proj[:, T1:T1 + T2, 1]
        vp = proj[:, T1 + T2:, 2]
        scores = jnp.einsum('bqhd,bkhd->bhqk', qp, kp) / np.sqrt(dh).astype(qp.dtype)
        mask = key_padding_mask[:, None, None, :] | attn_mask[None, None, :, :]
        scores = jnp.where(mask, NEG, scores)
        attn = jax.nn.softmax(scores, axis=-1)
        y = jnp.einsum('bhqk,bkhd->bqhd', attn, vp)
        y = y.reshape(Bq, T1, Dm)
        return y @ Wo + bo

    def _L3_ffn_ref(x, Wg, bg, W1, b1, W2, b2):
        import jax, jax.numpy as jnp
        import numpy as np
        D = 256
        E = 8
        N, T, d = x.shape
        x_flat = x.reshape(N * T, d)
        logits = x_flat @ Wg + bg
        probs = jax.nn.softmax(logits, axis=-1)
        assignments = jnp.argmax(probs, axis=-1)
        h = jnp.einsum('nd,edh->neh', x_flat, W1) + b1[None]
        h = jax.nn.gelu(h, approximate=False)
        eo = jnp.einsum('neh,ehd->ned', h, W2) + b2[None]
        selected = jnp.take_along_axis(eo, assignments[:, None, None], axis=1)[:, 0, :]
        w = jnp.take_along_axis(probs, assignments[:, None], axis=1)
        out = (w * selected).reshape(N, T, d)
        return out
    x = x + _L0_xattn_ref(_layernorm(x, axis=-1), ctx_1024, ctx_1024, mask_BxS2x1_ff1, L0_xattn_Wk, L0_xattn_Wv, L0_xattn_Wq, L0_xattn_Wo)
    x = x + _L0_ffn_ref(_layernorm(x, axis=-1), L0_ffn_W_in, L0_ffn_b_in, L0_ffn_W_out)
    x = x + _L1_xattn_ref(ctx_1024, ctx_1024, _layernorm(x, axis=-1), mask_Bx1xSxS2_ik1, L1_xattn_Wv, L1_xattn_Wk, L1_xattn_Wq)
    x = x + _L1_ffn_ref(_layernorm(x, axis=-1), L1_ffn_w1, L1_ffn_conv_w, L1_ffn_conv_b, L1_ffn_w2)
    x = x + _L2_xattn_ref(_layernorm(x, axis=-1), ctx_1024, ctx_1024, mask_Bx1xSxS2_ik1, L2_xattn_wq, L2_xattn_bq, L2_xattn_wk, L2_xattn_bk, L2_xattn_wv, L2_xattn_bv, L2_xattn_wo, L2_xattn_bo)
    x = x + _L2_ffn_ref(_layernorm(x, axis=-1), L2_ffn_w1_w, L2_ffn_w1_s, L2_ffn_w2_w, L2_ffn_w2_s, L2_ffn_h1_w, L2_ffn_h1_s, L2_ffn_h2_w, L2_ffn_h2_s, L2_ffn_w3_w, L2_ffn_w3_s)
    x = x + _L3_xattn_ref(_layernorm(x, axis=-1), ctx_1024, ctx_1024, L3_xattn_Wqkv, L3_xattn_bqkv, L3_xattn_Wo, L3_xattn_bo, mask_BxS2_bk0, mask_SxS2_bk1, 32)
    x = x + _L3_ffn_ref(_layernorm(x, axis=-1), L3_ffn_Wg, L3_ffn_bg, L3_ffn_W1, L3_ffn_b1, L3_ffn_W2, L3_ffn_b2)
    return x

_drawn_inputs = setup_inputs


def setup_inputs(seed=0):
    import zlib

    import numpy as np

    out = dict(_drawn_inputs(seed))
    spreads = {'L2_xattn_bq': (0.0, 0.1),
     'L2_xattn_bk': (0.0, 0.1),
     'L2_xattn_bv': (0.0, 0.1),
     'L2_xattn_bo': (0.0, 0.1)}
    factors = {}
    for name, (base, spread) in spreads.items():
        noise = np.random.default_rng([zlib.crc32(name.encode()), seed]).standard_normal(out[name].shape)
        drawn = base * np.exp(spread * noise) if base else spread * noise
        out[name] = jnp.asarray(drawn.astype(out[name].dtype))
    for name, factor in factors.items():
        out[name] = (out[name] * factor).astype(out[name].dtype)
    return out
```

```python
from contextlib import ExitStack

import concourse.bass as bass
from concourse import mybir

F32 = mybir.dt.float32
BF16 = mybir.dt.bfloat16
F16 = mybir.dt.float16
I32 = mybir.dt.int32
U8 = mybir.dt.uint8
ALU = mybir.AluOpType
ACT = mybir.ActivationFunctionType
AX = mybir.AxisListType
ds = bass.ds

B, S, D, SK = 8, 256, 256, 120
NT = B * S // 128
PAIRS = B // 2
TT = NT // PAIRS
TOK = TT * 128
K2 = D // 128
TREES, NODES = 8, 255
INNER, LEAVES = 127, 128
HID = 1024
HT = HID // 128
NE = 8
LN_EPS = 1e-5
MAGIC = 12582912.0
NEG_WHERE = -1e20
NEG_ADD = -1e9


class Layer:

    def __init__(self, name, phase, order, heads, scale):
        self.name, self.phase, self.order, self.heads, self.scale = name, phase, order, heads, scale
        self.dh = D // heads
        self.hg = 64 // self.dh
        self.sets = heads // 8
        self.pvh = heads // 2
        self.units = heads
        self.approx = TT * heads // 4


L1X = Layer("l1x", 2, 1, 16, 1.0 / 16.0)
L2X = Layer("l2x", 4, 2, 16, 0.25)
L3X = Layer("l3x", 6, 3, 32, 8.0 ** -0.5)
LAYERS = (L1X, L2X, L3X)


class Signals:
    pass


def build(nc, a, out, phases=8):
    es = ExitStack()
    base = nc.sbuf_base
    limit = nc.sbuf_usable_end
    cursor = [(base + 31) // 32 * 32]

    def size(shape, dt):
        n = 1
        for s in shape[1:]:
            n *= s
        return (n * mybir.dt.size(dt) + 31) // 32 * 32

    def put(name, shape, dt, at=None):
        at = cursor if at is None else at
        t = nc.alloc_sbuf_tensor_at(name, shape, dt, offset=at[0])
        at[0] += size(shape, dt)
        assert at[0] <= limit, (name, at[0], limit)
        return t

    x = put("x", [128, NT, D], F32)
    xln = put("xln", [128, TT, D], F32)
    xT = put("xT", [128, K2, TOK], F32)
    ctxp = put("ctxp", [128, K2, 2 * SK], F32)
    m32 = put("m32", [128, TT, SK], I32)
    ident = put("ident", [128, 128], F32)
    identb = put("identb", [128, 128], BF16)
    ones = put("ones", [128, 128], F32)
    selm = put("selm", [128, SK], BF16)
    sels = put("sels", [128, 8, SK], BF16)
    rev = put("rev", [128, NE], F32)
    rm8 = put("rm8", [128, 8], F32)
    rm4 = put("rm4", [128, 4], F32)
    stats = put("stats", [128, TT, 6], F32)
    mv = put("mv", [128, TT, 2], F32)
    veps = put("veps", [128, TT], F32)
    rstd = put("rstd", [128, TT], F32)
    mhalf = put("mhalf", [128, TT], F32)
    ceps = put("ceps", [128, TT], F32)
    tokm = put("tokm", [128, B], F32)
    negb = put("negb", [128, TREES], F32)
    bin2 = put("bin2", [128, TREES, 2], F32)
    tgt = put("tgt", [128, 2], F32)
    anc = put("anc", [128, 2, 128], BF16)
    r1 = cursor[0]
    at = [r1]
    wkvo = put("wkvo", [128, K2, 512], F32, at)
    wqT0 = put("wqT0", [128, K2, D], F32, at)
    winT = put("winT", [128, K2, TREES * NODES], F32, at)
    woutT = put("woutT", [128, 2 * TREES, D], F32, at)
    end1 = at[0]
    at = [r1]
    wq3 = put("wq3", [128, K2, D], F32, at)
    wk3 = put("wk3", [128, K2, 2 * D], F32, at)
    wv3 = put("wv3", [128, K2, D], F32, at)
    wo3 = put("wo3", [128, K2, D], F32, at)
    w1e = put("w1e", [128, NE, K2, D], F32, at)
    w2e = put("w2e", [128, NE, K2, D], F32, at)
    wg = put("wg", [128, K2, NE], F32, at)
    b2e = put("b2e", [8, D], F32, at)
    b1e = put("b1e", [128, NE, K2], F32, at)
    bgB = put("bgB", [128, NE], F32, at)
    r2 = max(end1, at[0])
    at = [r2]
    bdq = put("bdq", [128, 128], F32, at)
    bdk = put("bdk", [128, 2, 128], F32, at)
    bdv = put("bdv", [128, 128], F32, at)
    w1q = put("w1q", [128, K2, HID], BF16, at)
    w2q = put("w2q", [128, HT, D], BF16, at)
    cw = put("cw", [128, HT, 3], F32, at)
    cb = put("cb", [128, HT], F32, at)
    ws = put("ws", [128, 2], F32, at)
    r3 = at[0]
    at = [r3]
    wq2 = put("wq2", [128, K2, D], F32, at)
    wk2 = put("wk2", [128, K2, 2 * D], F32, at)
    wv2 = put("wv2", [128, K2, D], F32, at)
    wo2 = put("wo2", [128, K2, D], F32, at)
    f1 = put("f1", [128, K2, HID], F32, at)
    f2 = put("f2", [128, K2, HID], F32, at)
    f3 = put("f3", [128, HT, D], F32, at)
    bias2 = put("bias2", [128, 12], F32, at)
    bvB = put("bvB", [128, 2, D], F32, at)
    boB = put("boB", [128, 2, D], F32, at)
    s12 = put("s12", [128, 4, HT], F32, at)
    s3B = put("s3B", [128, D], F32, at)
    kpm = put("kpm", [128, B, SK], U8, at)
    attnm = put("attnm", [128, 2, SK], U8, at)
    r4 = at[0]
    at = [r4]
    h1w = put("h1w", [128, HT, HID], F32, at)
    h2w = put("h2w", [128, HT, HID], F32, at)
    r5 = at[0]
    at = [r5]
    ha = put("ha", [128, HT, TOK], F32, at)

    at = [r4]
    stage_wvT = put("stage_wvT", [128, K2, D], F32, at)
    stage_wo = put("stage_wo", [128, K2, D], F32, at)
    stage_w1 = put("stage_w1", [128, K2 * HID], F32, at)
    stage_w2 = put("stage_w2", [128, HT * D], F32, at)
    stage_sum = put("stage_sum", [128, 2], F32, at)
    stage_mean = put("stage_mean", [128, 2], F32, at)
    stage_ws = put("stage_ws", [128, 2], F32, at)
    anc_in = put("anc_in", [128, 2, 128], F32, at)
    sel_in = put("sel_in", [128, 8, SK], F32, at)
    dec0 = put("dec0", [128, 2, TOK], BF16, at)
    at = [r5]
    pk = put("pk", [SK, 2, D], F32, at)
    pvo = put("pvo", [SK, 2, D], F32, at)
    kvoS = put("kvoS", [128, 2, K2, D], F32, at)
    gS = put("gS", [128, 2, K2, D], F32, at)
    at = [r5]
    act0 = put("act0", [128, 2, 2, TOK], F32, at)
    msk0 = put("msk0", [128, 2, 2, TOK], F32, at)
    at = [r4]
    mtmp = put("mtmp", [128, TT, SK], BF16, at)
    MB = put("MB", [128, TT, 4, 128], BF16, at)
    MBT = put("MBT", [128, 4, TOK], BF16, at)
    Q2 = put("Q2", [128, 4, TOK], F16, at)
    k32 = put("k32", [128, 4, 2 * SK], F32, at)
    khi = put("khi", [128, 4, 2 * SK], F16, at)
    klo = put("klo", [128, 4, 2 * SK], F16, at)
    v32 = put("v32", [SK, 2, D], F32, at)
    V2 = put("V2", [SK, 2 * 16 * 2 * 17 + 1024], F16, at)
    e32 = put("e32", [SK, 3, 512], F32, at)
    phi = put("phi", [SK, 3, 512], F16, at)
    plo = put("plo", [SK, 3, 512], F16, at)
    pn = put("pn", [128, 2, 16 * 17], F32, at)
    rden = put("rden", [128, 2, 16], F32, at)
    o = put("o", [128, TT, D], F32, at)
    oT = put("oT", [128, K2, TOK], F32, at)
    Kpad = put("Kpad", [128, 2, 8, 4, 2 * SK], F16, at)
    at = [r4]
    amax = put("amax", [128, TT], F32, at)
    qsc = put("qsc", [128, 2, TT], F32, at)
    sdq = put("sdq", [128, 2, TT], F32, at)
    xr = put("xr", [128, TT, D], F32, at)
    xq = put("xq", [128, TT, D], BF16, at)
    xqT = put("xqT", [128, K2, TOK], BF16, at)
    dg = put("dg", [128, TT, 128], F32, at)
    sB = put("sB", [128, TOK], F32, at)
    hpad = put("hpad", [128, 2, 2, S + 2], F32, at)
    yc = put("yc", [128, 3, TOK], F32, at)
    mpart = put("mpart", [128, 2, TOK], F32, at)
    mrun = put("mrun", [128, TOK], F32, at)
    hq = put("hq", [128, HT, TOK], BF16, at)
    hr = put("hr", [128, 2, TOK], F32, at)
    at = [r1]
    sg = put("sg", [128, 2, TOK], F32, at)
    xsc = put("xsc", [128, 2, D], F32, at)
    hb = put("hb", [128, HT, TOK], F32, at)
    at = [r5]
    he = put("he", [128, 2, K2, TOK], F32, at)
    gl = put("gl", [128, TT, NE], F32, at)
    gmx = put("gmx", [128, TT], F32, at)
    gex = put("gex", [128, TT, NE], F32, at)
    gsum = put("gsum", [128, TT], F32, at)
    grc = put("grc", [128, TT], F32, at)
    gv = put("gv", [128, TT, NE], F32, at)
    gwt = put("gwt", [128, TT, NE], F32, at)
    gT = put("gT", [NE, TOK], F32, at)

    bank = [es.enter_context(nc.psum_tensor(f"bank{b}", [128, 512], F32)) for b in range(8)]
    bankh = [t[:, :].bitcast(BF16) for t in bank]

    def sem(name):
        return es.enter_context(nc.semaphore(name))

    ld_x, ld_const, ld_l0, ld_in, ld_out_w, ld_l1, ld_l2, ld_h, ld_l3 = (
        sem(n) for n in ("ld_x", "ld_const", "ld_l0", "ld_in", "ld_out_w", "ld_l1", "ld_l2", "ld_h", "ld_l3"))
    ld_anc = sem("ld_anc")
    ctx_ready, mask_ready, stored = sem("ctx_ready"), sem("mask_ready"), sem("stored")
    filled, wvo_ps, wvo_done, wsum, wsum_ps, wmean, wrcp, consts, bias_done = (
        sem(n) for n in ("filled", "wvo_ps", "wvo_done", "wsum", "wsum_ps", "wmean", "wrcp", "consts", "bias_done"))
    ln_var, ln_rstd, xln_ready, xT_ps, xT_ready, res_done = (
        sem(n) for n in ("ln_var", "ln_rstd", "xln_ready", "xT_ps", "xT_ready", "res_done"))
    A = Signals()
    A.kv, A.pk, A.pvo, A.kvo, A.kvoS, A.g, A.gS, A.out = (
        sem("a_" + n) for n in ("kv", "pk", "pvo", "kvo", "kvoS", "g", "gS", "out"))
    Bf = Signals()
    Bf.logits, Bf.dec, Bf.act, Bf.cnt, Bf.msk, Bf.out = (
        sem("b_" + n) for n in ("logits", "dec", "act", "cnt", "msk", "out"))
    Ff = Signals()
    Ff.gate, Ff.silu, Ff.h0, Ff.p1, Ff.h1, Ff.p2, Ff.h2, Ff.out = (
        sem("f_" + n) for n in ("gate", "silu", "h0", "p1", "h1", "p2", "h2", "out"))
    Df = Signals()
    Df.xq, Df.xqt, Df.xqT, Df.sb, Df.sB, Df.up, Df.deq, Df.mid, Df.conv = (
        sem("d_" + n) for n in ("xq", "xqt", "xqT", "sb", "sB", "up", "deq", "mid", "conv"))
    Df.silu, Df.mrun, Df.mt, Df.dgh, Df.qb, Df.hq, Df.out = (
        sem("d_" + n) for n in ("silu", "mrun", "mt", "dgh", "qb", "hq", "out"))
    Hf = Signals()
    Hf.lg, Hf.gl, Hf.gex, Hf.gw, Hf.gt, Hf.gT, Hf.up, Hf.he, Hf.eo = (
        sem("h_" + n) for n in ("lg", "gl", "gex", "gw", "gt", "gT", "up", "he", "eo"))
    Hf.acc = sem("h_acc")
    X = {}
    for L in LAYERS:
        s = Signals()
        s.kp, s.vp, s.qp, s.k32, s.v32, s.qhi, s.kpad, s.v2, s.qlo = (
            sem(L.name + "_" + n) for n in ("kp", "vp", "qp", "k32", "v32", "qhi", "kpad", "v2", "qlo"))
        s.mb, s.ap, s.red, s.mt, s.mbt, s.sc, s.exp, s.phi, s.lo = (
            sem(L.name + "_" + n) for n in ("mb", "ap", "red", "mt", "mbt", "sc", "exp", "phi", "lo"))
        s.pv, s.pvc, s.o, s.oT, s.oTs, s.out, s.bo = (
            sem(L.name + "_" + n) for n in ("pv", "pvc", "o", "oT", "oTs", "out", "bo"))
        X[L.name] = s

    def next_pair(i):
        return (i + 1) % PAIRS

    def rows(i, n=TT):
        return x[:, ds(TT * i, n), :]

    def v2(L, b):
        w = L.heads * 2 * (L.dh + 1)
        return V2[:, b * w:(b + 1) * w].rearrange("p (h v d) -> p h v d", h=L.heads, v=2)

    proj = {"l1x": None, "l2x": (wq2, wk2, wv2, wo2), "l3x": (wq3, wk3, wv3, wo3)}
    LD_CONST, LD_L0, LD_IN, LD_OUT, LD_L1 = 6 * 16, 4 * 16, 2 * 16, 2 * 16, 7 * 16
    LD_L2, LD_H, LD_L3 = (7 + 3 + 2 * 2 + 2) * 16, 2 * 16, (4 + 2 + 2 + 2) * 16
    block = es.enter_context(nc.Block())

    @block.sync
    def _(sp):
        kp = lambda t: t.rearrange("(k p) n -> p k n", p=128)
        sp.dma_start(x[:], a["x"].rearrange("(t p) d -> p t d", p=128)).then_inc(ld_x, 16)
        sp.dma_start(ident[:], a["ident"]).then_inc(ld_const, 16)
        sp.dma_start(tokm[0:SK, :], a["tokm"]).then_inc(ld_const, 16)
        sp.dma_start(rm4[:], a["rm4"]).then_inc(ld_const, 16)
        sp.dma_start(rm8[:], a["rm8"]).then_inc(ld_const, 16)
        sp.dma_start(rev[:], a["rev"]).then_inc(ld_const, 16)
        sp.dma_start(tgt[:], a["tgt"]).then_inc(ld_const, 16)
        sp.dma_start(ctxp[:], kp(a["ctxT"][:, 0:2 * SK])).then_inc(ctx_ready, 16)
        sp.dma_start(wkvo[:, :, 0:D], kp(a["wk0"])).then_inc(ld_l0, 16)
        sp.dma_start(wqT0[:], kp(a["wqT0"])).then_inc(ld_l0, 16)
        sp.dma_start(stage_wvT[:], kp(a["wvT0"])).then_inc(ld_l0, 16)
        sp.dma_start(stage_wo[:], kp(a["wo0"])).then_inc(ld_l0, 16)
        sp.dma_start(winT[:], kp(a["winT"])).then_inc(ld_in, 16)
        sp.dma_start(bin2[:].rearrange("p t c -> p (t c)"), a["bin2"]).then_inc(ld_in, 16)
        for c, n in ((0, INNER), (1, LEAVES)):
            src = a["woutT"].rearrange("(t n) d -> n t d", n=NODES)[INNER * c:INNER * c + n]
            sp.dma_start(woutT[0:n, c::2, :], src).then_inc(ld_out_w, 16)
        sp.dma_start(stage_w1[:].rearrange("p (k n) -> p k n", k=K2), kp(a["w1T"])).then_inc(ld_l1, 16)
        sp.dma_start(stage_w2[:].rearrange("p (k n) -> p k n", k=HT), kp(a["w2T"])).then_inc(ld_l1, 16)
        sp.dma_start(cw[:].rearrange("p t c -> p (t c)"), a["cw"]).then_inc(ld_l1, 16)
        sp.dma_start(cb[:], a["cb"]).then_inc(ld_l1, 16)
        for w, bd in (("bdq", bdq), ("bdk", bdk), ("bdv", bdv)):
            sp.dma_start(bd[:] if bd is not bdk else bd[:].rearrange("p h n -> p (h n)"), a[w]).then_inc(ld_l1, 16)
        for t, w in ((wq2, "wq2"), (wk2, "wk2"), (wv2, "wv2"), (wo2, "wo2"), (f1, "f1T"), (f2, "f2T"), (f3, "f3T")):
            sp.dma_start(t[:], kp(a[w])).then_inc(ld_l2, 16)
        sp.dma_start(s12[:].rearrange("p n t -> p (n t)"), a["s12"]).then_inc(ld_l2, 16)
        sp.dma_start(bias2[:], a["bias2"]).then_inc(ld_l2, 16)
        sp.dma_start(s3B[:], a["w3_s"].partition_broadcast(128)).then_inc(ld_l2, 16)
        for n, c in ((0, "2"), (1, "3")):
            sp.dma_start(bvB[:, n, :], a["bv" + c].partition_broadcast(128)).then_inc(ld_l2, 16)
            sp.dma_start(boB[:, n, :], a["bo" + c].partition_broadcast(128)).then_inc(ld_l2, 16)
        sp.dma_start(kpm[:], a["kpm"].rearrange("b k -> (b k)").partition_broadcast(128)).then_inc(ld_l2, 16)
        sp.dma_start(attnm[:], a["attnm"].rearrange("(t p) k -> p t k", p=128)).then_inc(ld_l2, 16)

        def next_context(i):
            sp.dma_start(ctxp[:], kp(a["ctxT"][:, ds(next_pair(i) * (2 * SK), 2 * SK)])).then_inc(ctx_ready, 16)

        with sp.Fori(0, PAIRS) as i:
            sp.wait_ge(A.kv, i * 2 + 2)
            next_context(i)
        for L in LAYERS:
            if phases <= L.phase:
                break
            s = X[L.name]
            sp.wait_ge(res_done, 4 * L.phase + 1)
            sp.wait_ge(wrcp, 1)
            if L is L3X:
                sp.dma_start(wq3[:], kp(a["wq3"])).then_inc(ld_l3, 16)
                sp.dma_start(wk3[:], kp(a["wk3"])).then_inc(ld_l3, 16)
                sp.dma_start(wv3[:], kp(a["wv3"])).then_inc(ld_l3, 16)
                sp.dma_start(wo3[:], kp(a["wo3"])).then_inc(ld_l3, 16)
                sp.dma_start(w1e[:], a["w1e"].rearrange("e (k p) n -> p e k n", p=128)).then_inc(ld_l3, 16)
                sp.dma_start(w2e[:], a["w2e"].rearrange("e (k p) n -> p e k n", p=128)).then_inc(ld_l3, 16)
                sp.dma_start(wg[:], kp(a["wg"])).then_inc(ld_l3, 16)
                sp.dma_start(b2e[:], a["b2e"]).then_inc(ld_l3, 16)
                sp.dma_start(b1e[:].rearrange("p e k -> p (e k)"), a["b1e"]).then_inc(ld_l3, 16)
                sp.dma_start(bgB[:], a["bg"].partition_broadcast(128)).then_inc(ld_l3, 16)
            elif L is L1X:
                sp.dma_start(m32[:], a["mask"][0:TOK, :].rearrange("(t p) k -> p t k", p=128)).then_inc(mask_ready, 16)
            with sp.Fori(0, PAIRS) as i:
                if L is not L3X:
                    sp.wait_ge(s.mb, i + 1)
                    sp.dma_start(m32[:], a["mask"][ds(next_pair(i) * TOK, TOK), :]
                                 .rearrange("(t p) k -> p t k", p=128)).then_inc(mask_ready, 16)
                sp.wait_ge(s.kp, i + 1)
                sp.wait_ge(s.vp, i + 1)
                next_context(i)
            if L is L2X and phases > 5:
                sp.wait_ge(mask_ready, 16 * 9)
                sp.wait_ge(res_done, 4 * 5 + 1)
                sp.dma_start(h1w[:], kp(a["h1T"])).then_inc(ld_h, 16)
                sp.dma_start(h2w[:], kp(a["h2T"])).then_inc(ld_h, 16)
        for load, total in ((ld_x, 16), (ld_const, LD_CONST), (ld_l0, LD_L0), (ld_in, LD_IN), (ld_out_w, LD_OUT),
                            (ld_l1, LD_L1), (ld_l2, LD_L2), (ld_anc, 32), (mask_ready, (0, 16 * 5, 16 * 9)[sum(phases > q for q in (2, 4))]),
                            (ld_h, LD_H if phases > 5 else 0), (ld_l3, LD_L3 if phases > 6 else 0),
                            (ctx_ready, 16 + 64 * sum(phases > q for q in (0, 2, 4, 6)))):
            if total:
                sp.wait_ge(load, total)
        sp.wait_ge(res_done, 4 * phases + 1)
        sp.dma_start(out.rearrange("(t p) d -> p t d", p=128), x[:]).then_inc(stored, 16)
        sp.wait_ge(stored, 16)

    @block.gpsimd
    def _(pool):
        pool.memset(mhalf[:], -0.5)
        pool.memset(ceps[:], LN_EPS)
        pool.memset(ones[:], 1.0)
        pool.drain().then_inc(filled, 1)
        pool.sem_inc(res_done, 1)

        def rstd_of(n):
            pool.wait_ge(ln_var, n)
            pool.tensor_tensor(veps[:], mv[:, :, 1], ceps[:], ALU.add)
            pool.drain()
            pool.tensor_tensor(rstd[:], veps[:], mhalf[:], ALU.pow).then_inc(ln_rstd, 1)

        rstd_of(1)

        for p in range(phases):
            with pool.Fori(0, PAIRS) as i:
                if p in (4, 6):
                    if p == 4:
                        pool.wait_ge(ld_l2, LD_L2)
                    pool.wait_ge(xln_ready, 4 * p + i + 1)
                    pool.tensor_tensor(rows(i), rows(i), boB[:, p // 2 - 2, :].unsqueeze(1).broadcast_to([128, TT, D]),
                                       ALU.add).then_inc(X["l2x" if p == 4 else "l3x"].bo, 1)
                rstd_of(i + (4 * p + 2))

    @block.vector
    def _(dve):
        def ln_stats(pair, n):
            for t in range(TT):
                dve.bn_stats(stats[:, t, :], x[:, ds(TT * pair + t, 1), :].rearrange("p t d -> p (t d)"))
            dve.drain()
            for t in range(TT):
                dve.bn_aggr(mv[:, t, :], stats[:, t, :])
            dve.drain().then_inc(ln_var, 1)

        def ln_rows(pair, n):
            dve.wait_ge(ln_rstd, n)
            for t in range(TT):
                dve.tensor_scalar(xln[:, t, :], x[:, ds(TT * pair + t, 1), :].rearrange("p t d -> p (t d)"),
                                  mv[:, t, 0:1], rstd[:, t:t + 1], ALU.subtract, ALU.mult)
            dve.drain().then_inc(xln_ready, 1)

        def norm_stats(p, i):
            dve.drain()
            ln_stats(next_pair(i), None)

        def norm_rows(p, i):
            dve.wait_ge(xT_ps, 4 * p + i + 1)
            ln_rows(next_pair(i), i + (4 * p + 2))

        def residual(i, half, ps):
            xs = x[:, ds(TT * i + 2 * half, 2), :].rearrange("p t d -> p (t d)")
            return dve.tensor_tensor(xs, xs, ps, ALU.add)

        dve.wait_ge(ld_x, 16)
        ln_stats(0, 1)
        ln_rows(0, 1)
        dve.wait_ge(ld_const, LD_CONST)
        dve.tensor_copy(identb[:], ident[:])
        dve.tensor_copy(selm[:], ident[:, 0:SK])
        dve.wait_ge(ld_anc, 32)
        dve.tensor_copy(anc[:], anc_in[:])
        dve.tensor_copy(sels[:], sel_in[:])
        dve.drain().then_inc(consts, 1)
        dve.wait_ge(wvo_ps, 1)
        dve.tensor_copy(wkvo[:, :, D:2 * D], bank[0][:, :].rearrange("p (k n) -> p k n", k=K2)).then_inc(wvo_done, 1)

        def round_weights():
            dve.wait_ge(ld_l1, LD_L1)
            dve.tensor_reduce(stage_sum[:, 0:1], stage_w1[:], AX.X, ALU.add, apply_absolute_value=True)
            dve.tensor_reduce(stage_sum[:, 1:2], stage_w2[:], AX.X, ALU.add, apply_absolute_value=True)
            dve.drain().then_inc(wsum, 1)
            dve.wait_ge(wsum_ps, 1)
            dve.tensor_scalar(ws[:], bank[1][:, 0:2], 1.0 / (D * HID), 1e-5, ALU.mult, ALU.max)
            dve.drain()
            dve.reciprocal(stage_ws[:], ws[:])
            dve.drain()
            for n, (st, q) in enumerate(((stage_w1, w1q), (stage_w2, w2q))):
                flat = q[:].rearrange("p k n -> p (k n)")
                dve.tensor_scalar(st[:], st[:], stage_ws[:, n:n + 1], MAGIC, ALU.mult, ALU.add)
                dve.drain()
                dve.tensor_scalar(st[:], st[:], MAGIC - 1, MAGIC + 1, ALU.max, ALU.min)
                dve.drain()
                dve.tensor_scalar(flat, st[:], MAGIC, None, ALU.subtract)
            dve.tensor_scalar(cw[:], cw[:], ws[:, 0:1], None, ALU.mult)
            dve.drain().then_inc(wrcp, 1)

        if phases > 0:
            with dve.Fori(0, PAIRS) as i:
                norm_stats(0, i)
                for j in range(2):
                    dve.wait_ge(A.pk, i * 2 + (j + 1))
                    dve.tensor_scalar(pvo[:, j, :], bank[j][0:SK, D:2 * D], tokm[0:SK, ds(i * 2 + j, 1)], None,
                                      ALU.mult).then_inc(A.pvo, 1)
                norm_rows(0, i)
                for j in range(2):
                    dve.wait_ge(A.g, i * 2 + (j + 1))
                    dve.tensor_copy(gS[:, j, :, :].rearrange("p k n -> p (k n)"), bank[j][:, :]).then_inc(A.gS, 1)
                for h in range(2):
                    dve.wait_ge(A.out, i * 2 + (h + 1))
                    residual(i, h, bank[4 + h][:, :])
                dve.drain().then_inc(res_done, 1)

        if phases > 1:
            dve.wait_ge(ld_in, LD_IN)
            dve.tensor_scalar(negb[0:INNER, :], bin2[0:INNER, :, 0], -1.0, None, ALU.mult)
            dve.drain()
            with dve.Fori(0, PAIRS) as i:
                def masked(p):
                    dve.wait_ge(Bf.cnt, i * TREES + (p + 1))
                    for c, n in ((0, INNER), (1, LEAVES)):
                        dve.wait_ge(Bf.act, i * (2 * TREES) + (2 * p + c + 1))
                        dve.scalar_tensor_tensor(out=msk0[0:n, p % 2, c, :], in0=bank[6 + c][0:n, :],
                                                 scalar=tgt[0:n, c:c + 1], in1=act0[0:n, p % 2, c, :],
                                                 op0=ALU.is_equal, op1=ALU.mult).then_inc(Bf.msk, 1)

                for p in range(TREES):
                    dve.wait_ge(Bf.logits, i * (2 * TREES) + (2 * p + 1))
                    dve.tensor_scalar(dec0[0:INNER, p % 2, :], bank[2 + 2 * (p % 2)][0:INNER, :],
                                      negb[0:INNER, p:p + 1], None, ALU.is_gt).then_inc(Bf.dec, 1)
                    if p >= 1:
                        masked(p - 1)
                    if p == 2:
                        norm_stats(1, i)
                    if p == 3:
                        norm_rows(1, i)
                masked(TREES - 1)
                dve.wait_ge(Bf.out, i + 1)
                for h in range(2):
                    residual(i, h, bank[h][:, :])
                dve.drain().then_inc(res_done, 1)

        def attention(L):
            s, HG, dh, ph = X[L.name], L.hg, L.dh, L.phase
            dve.wait_ge(res_done, 4 * ph + 1)
            dve.memset(V2[:], 0.0)
            dve.drain()
            for b in range(2):
                dve.memset(v2(L, b)[:, :, 0, dh:dh + 1], 1.0)
            dve.drain()
            n_units, n_ap = L.units, L.approx
            with dve.Fori(0, PAIRS) as i:
                norm_stats(ph, i)
                if L is L3X:
                    kp_ = kpm[:, ds(i * 2, 2), :].unsqueeze(2).broadcast_to([128, 2, 2, SK])
                    at_ = attnm[:].unsqueeze(1).broadcast_to([128, 2, 2, SK])
                    dve.tensor_tensor(mtmp[:].rearrange("p (b t) k -> p b t k", b=2), kp_, at_, ALU.max)
                    dve.drain()
                    for h in range(L.sets):
                        dve.tensor_scalar(MB[:, :, h, 0:SK], mtmp[:], NEG_WHERE, None, ALU.mult)
                else:
                    dve.wait_ge(mask_ready, i * 16 + 16 * (1 if L is L1X else 5))
                    for h in range(L.sets):
                        if L is L1X:
                            dve.tensor_scalar(MB[:, :, h, 0:SK], m32[:], 0.0, NEG_WHERE, ALU.is_equal, ALU.mult)
                        else:
                            dve.tensor_scalar(MB[:, :, h, 0:SK], m32[:], NEG_ADD, None, ALU.mult)
                dve.drain().then_inc(s.mb, 1)
                dve.wait_ge(s.k32, i + 1)
                dve.tensor_copy(khi[:], k32[:])
                dve.drain()
                dve.tensor_tensor(klo[:], k32[:], khi[:], ALU.subtract)
                rm = rm4 if HG == 4 else rm8
                for v, kk in ((0, khi), (1, klo)):
                    if v:
                        dve.drain()
                    for r in range(HG):
                        dve.tensor_scalar(Kpad[:, v, r, :, :], kk[:], rm[:, r:r + 1], None, ALU.mult)
                dve.drain().then_inc(s.kpad, 1)
                for g in range(4):
                    f, half = g // 2, g % 2
                    src = slice(64 * half, 64 * half + 64)
                    dst = slice(64 - 64 * half, 128 - 64 * half)
                    dve.wait_ge(s.qhi, i * 4 + (g + 1))
                    if L is L1X:
                        last = dve.tensor_tensor(Q2[dst, g, :], bank[f][src, :], Q2[src, g, :], ALU.subtract)
                    else:
                        c = 6 * (L.order - 2) + f
                        last = dve.scalar_tensor_tensor(out=Q2[dst, g, :], in0=bank[f][src, :],
                                                        scalar=bias2[src, c:c + 1], in1=Q2[src, g, :],
                                                        op0=ALU.add, op1=ALU.subtract)
                last.then_inc(s.qlo, 1)
                if L is L1X:
                    dve.wait_ge(s.v32, i + 1)
                else:
                    dve.wait_ge(s.vp, i + 1)
                    dve.tensor_tensor(v32[:], bank[4][0:SK, :].rearrange("p (b n) -> p b n", b=2),
                                      bvB[0:SK, L.order - 2, :].unsqueeze(1).broadcast_to([SK, 2, D]), ALU.add)
                    dve.drain()
                for b in range(2):
                    vh = v32[:, b, :].rearrange("p (h d) -> p h d", d=dh)
                    dve.tensor_copy(v2(L, b)[:, :, 0, 0:dh], vh)
                dve.drain()
                for b in range(2):
                    vh = v32[:, b, :].rearrange("p (h d) -> p h d", d=dh)
                    dve.tensor_tensor(v2(L, b)[:, :, 1, 0:dh], vh, v2(L, b)[:, :, 0, 0:dh], ALU.subtract)
                dve.drain().then_inc(s.v2, 1)
                norm_rows(ph, i)
                per = L.heads // 4
                for t in range(TT):
                    for q in range(per):
                        n = t * per + q
                        dve.wait_ge(s.ap, i * n_ap + (n + 1))
                        h0 = 4 * q
                        dve.tensor_reduce(MB[:, t, h0 // 8, SK + h0 % 8:SK + h0 % 8 + 4],
                                          bank[2 + n % 4][:, 0:4 * SK].rearrange("p (h k) -> p h k", h=4),
                                          AX.X, ALU.max).then_inc(s.red, 1)

                def consume(st):
                    b, w = st // 2, dh + 1
                    last_u = (st + 1) * n_units // 4
                    dve.wait_ge(s.pv, i * n_units + last_u)
                    banks = (0, 1) if st % 2 == 0 else (6, 7)
                    for q in range(2):
                        acc = bank[banks[q]][:, 0:L.pvh * 2 * w].rearrange("p (h v d) -> p h d v", h=L.pvh, v=2)
                        dve.tensor_reduce(pn[:, q, 0:L.pvh * w].rearrange("p (h d) -> p h d", h=L.pvh), acc,
                                          AX.X, ALU.add)
                    dve.drain().then_inc(s.pvc, 1)
                    nn = pn[:, :, 0:L.pvh * w].rearrange("p q (h d) -> p q h d", h=L.pvh)
                    dve.reciprocal(rden[:, :, 0:L.pvh], nn[:, :, :, dh])
                    dve.drain()
                    for q in range(2):
                        c0 = (st % 2) * (D // 2)
                        dve.tensor_tensor(o[:, 2 * b + q, c0:c0 + D // 2].rearrange("p (h d) -> p h d", d=dh),
                                          nn[:, q, :, 0:dh],
                                          rden[:, q, 0:L.pvh].unsqueeze(2).broadcast_to([128, L.pvh, dh]), ALU.mult)

                done = 0
                for u in range(n_units):
                    dve.wait_ge(s.phi, i * n_units + (u + 1))
                    dve.tensor_tensor(plo[:, u % 3, :], e32[:, u % 3, :], phi[:, u % 3, :],
                                      ALU.subtract).then_inc(s.lo, 1)
                    while done < 3 and u >= (done + 1) * n_units // 4 + 2:
                        consume(done)
                        done += 1
                while done < 4:
                    consume(done)
                    done += 1
                dve.drain().then_inc(s.o, 1)
                if L is L1X:
                    xs = rows(i)
                    dve.tensor_tensor(xs, xs, o[:], ALU.add)
                else:
                    dve.wait_ge(s.bo, i + 1)
                    dve.wait_ge(s.out, i + 1)
                    for h in range(2):
                        residual(i, h, bank[2 + h][:, :])
                dve.drain().then_inc(res_done, 1)

        if phases > 2:
            round_weights()
            attention(L1X)

        def quantiser(which):
            dve.tensor_scalar(amax[:], amax[:], 1e-5, None, ALU.max)
            dve.drain()
            dve.reciprocal(qsc[:, which, :], amax[:])
            dve.drain()
            dve.tensor_scalar(qsc[:, which, :], qsc[:, which, :], 127.0, None, ALU.mult)
            dve.drain()

        if phases > 3:
            dve.wait_ge(res_done, 4 * 3 + 1)
            for j in range(2):
                dve.memset(hpad[:, j, :, 0:1], 0.0)
                dve.memset(hpad[:, j, :, S + 1:S + 2], 0.0)
            with dve.Fori(0, PAIRS) as i:
                dve.drain()
                dve.tensor_reduce(amax[:], xln[:], AX.X, ALU.max, apply_absolute_value=True)
                dve.drain()
                quantiser(0)
                for t in range(TT):
                    dve.tensor_scalar(xr[:, t, :], xln[:, t, :], qsc[:, 0, t:t + 1], MAGIC, ALU.mult, ALU.add)
                dve.reciprocal(sdq[:, 0, :], qsc[:, 0, :])
                dve.drain()
                dve.tensor_scalar(xr[:], xr[:], MAGIC - 128, MAGIC + 127, ALU.max, ALU.min)
                for t in range(TT):
                    dve.tensor_scalar(dg[:, t, :], ident[:], sdq[:, 0, t:t + 1], None, ALU.mult)
                dve.drain()
                dve.tensor_scalar(xq[:], xr[:], MAGIC, None, ALU.subtract)
                dve.drain().then_inc(Df.xq, 1)
                norm_stats(3, i)
                norm_rows(3, i)
                def tail(t):
                    dve.wait_ge(Df.mid, i * HT + (t + 1))
                    y = yc[:, t % 3, :].rearrange("p (b s) -> p b s", b=2)
                    dve.scalar_tensor_tensor(out=y, in0=hpad[:, t % 2, :, 0:S], scalar=cw[:, t, 0:1], in1=y,
                                             op0=ALU.mult, op1=ALU.add)
                    dve.drain()
                    dve.scalar_tensor_tensor(out=y, in0=hpad[:, t % 2, :, 2:S + 2], scalar=cw[:, t, 2:3], in1=y,
                                             op0=ALU.mult, op1=ALU.add).then_inc(Df.conv, 1)

                def largest(q):
                    dve.wait_ge(Df.silu, i * HT + 4 * (q + 1))
                    dve.tensor_reduce(mpart[:, q, :], ha[:, 4 * q:4 * q + 4, :].rearrange("p t n -> p n t"), AX.X,
                                      ALU.max, apply_absolute_value=True)

                for t in range(HT):
                    dve.drain()
                    if t == 0:
                        dve.wait_ge(Df.sB, i + 1)
                    dve.wait_ge(Df.up, i * HT + (t + 1))
                    dve.tensor_tensor(hpad[:, t % 2, :, 1:S + 1], bank[t % 4][:, :].rearrange("p (b s) -> p b s", b=2),
                                      sB[:].rearrange("p (b s) -> p b s", b=2), ALU.mult).then_inc(Df.deq, 1)
                    if t >= 1:
                        tail(t - 1)
                    if t == 6:
                        largest(0)
                tail(HT - 1)
                largest(1)
                dve.drain()
                dve.tensor_tensor(mrun[:], mpart[:, 0, :], mpart[:, 1, :], ALU.max).then_inc(Df.mrun, 1)
                dve.wait_ge(Df.mt, i + 1)
                dve.tensor_reduce(amax[:], bank[4][:, :].rearrange("p (t n) -> p t n", t=TT), AX.X, ALU.max)
                dve.drain()
                quantiser(1)
                dve.reciprocal(sdq[:, 1, :], qsc[:, 1, :])
                for t in range(TT):
                    dve.tensor_scalar(dg[:, t, :], ident[:], qsc[:, 1, t:t + 1], None, ALU.mult)
                dve.drain().then_inc(Df.dgh, 1)
                dve.tensor_scalar(sdq[:, 1, :], sdq[:, 1, :], ws[:, 1:2], None, ALU.mult)
                dve.wait_ge(Df.qb, i + 1)
                for t in range(HT):
                    dve.tensor_tensor(ha[:, t, :], ha[:, t, :], bank[5][:, :], ALU.mult)
                    dve.drain()
                    dve.tensor_scalar(hr[:, t % 2, :], ha[:, t, :], MAGIC, MAGIC - 128, ALU.add, ALU.max)
                    dve.drain()
                    dve.tensor_scalar(hq[:, t, :], hr[:, t % 2, :], MAGIC + 127, MAGIC, ALU.min,
                                      ALU.subtract).then_inc(Df.hq, 1)
                dve.wait_ge(Df.out, i + 1)
                for t in range(TT):
                    xs = x[:, ds(TT * i + t, 1), :].rearrange("p t d -> p (t d)")
                    dve.scalar_tensor_tensor(out=xs, in0=bank[t // 2][:, (t % 2) * D:(t % 2) * D + D],
                                             scalar=sdq[:, 1, t:t + 1], in1=xs, op0=ALU.mult, op1=ALU.add)
                dve.drain().then_inc(res_done, 1)

        if phases > 4:
            dve.wait_ge(ld_l2, LD_L2)
            dve.tensor_scalar(bias2[:, 2:6], bias2[:, 2:6], L2X.scale, None, ALU.mult)
            dve.tensor_scalar(bias2[:, 8:12], bias2[:, 8:12], L3X.scale, None, ALU.mult)
            dve.drain().then_inc(bias_done, 1)
            attention(L2X)

        if phases > 5:
            with dve.Fori(0, PAIRS) as i:
                for t in range(HT):
                    dve.wait_ge(Ff.silu, i * HT + (t + 1))
                    dve.scalar_tensor_tensor(out=ha[:, t, :], in0=bank[2 * (t % 2) + 1][:, :],
                                             scalar=s12[:, 1, t:t + 1], in1=sg[:, t % 2, :], op0=ALU.mult,
                                             op1=ALU.mult).then_inc(Ff.h0, 1)
                norm_stats(5, i)
                norm_rows(5, i)
                for h in range(2):
                    dve.drain()
                    dve.wait_ge(Ff.out, i * 2 + (h + 1))
                    dve.tensor_tensor(xsc[:], bank[4 + h][:, :].rearrange("p (t d) -> p t d", t=2),
                                      s3B[:].unsqueeze(1).broadcast_to([128, 2, D]), ALU.mult)
                    dve.drain()
                    residual(i, h, xsc[:].rearrange("p t d -> p (t d)"))
                dve.drain().then_inc(res_done, 1)

        if phases > 6:
            attention(L3X)

        if phases > 7:
            with dve.Fori(0, PAIRS) as i:
                dve.wait_ge(Hf.lg, i + 1)
                dve.tensor_tensor(gl[:], bank[0][:, 0:TT * NE].rearrange("p (t e) -> p t e", t=TT),
                                  bgB[:].unsqueeze(1).broadcast_to([128, TT, NE]), ALU.add)
                dve.drain()
                dve.tensor_reduce(gmx[:], gl[:], AX.X, ALU.max)
                dve.drain()
                dve.tensor_tensor(gl[:], gl[:], gmx[:].unsqueeze(2).broadcast_to([128, TT, NE]),
                                  ALU.subtract).then_inc(Hf.gl, 1)
                norm_stats(7, i)
                dve.wait_ge(Hf.gex, i + 1)
                dve.tensor_reduce(gmx[:], gex[:], AX.X, ALU.max)
                dve.tensor_reduce(gsum[:], gex[:], AX.X, ALU.add)
                dve.drain()
                dve.reciprocal(grc[:], gsum[:])
                dve.tensor_tensor(gv[:], gex[:], gmx[:].unsqueeze(2).broadcast_to([128, TT, NE]), ALU.is_equal)
                dve.drain()
                dve.tensor_tensor(gv[:], gv[:], rev[:].unsqueeze(1).broadcast_to([128, TT, NE]), ALU.mult)
                dve.tensor_tensor(grc[:], grc[:], gmx[:], ALU.mult)
                dve.drain()
                dve.tensor_reduce(gsum[:], gv[:], AX.X, ALU.max)
                dve.drain()
                dve.tensor_tensor(gwt[:], gv[:], gsum[:].unsqueeze(2).broadcast_to([128, TT, NE]), ALU.is_equal)
                dve.drain()
                dve.tensor_tensor(gwt[:], gwt[:], grc[:].unsqueeze(2).broadcast_to([128, TT, NE]),
                                  ALU.mult).then_inc(Hf.gw, 1)
                norm_rows(7, i)
                for e in range(NE + 1):
                    for h in range(2):
                        n = 2 * e + h
                        dve.drain()
                        dve.wait_ge(Hf.eo, i * (2 * NE + 2) + (n + 1))
                        pb = bank[[4, 5, 2, 3][n % 4]]
                        if e < NE:
                            for q in range(2):
                                t = 2 * h + q
                                xs = x[:, ds(TT * i + t, 1), :].rearrange("p t d -> p (t d)")
                                last = dve.scalar_tensor_tensor(out=xs, in0=pb[:, q * D:q * D + D],
                                                                scalar=gwt[:, t, e:e + 1], in1=xs, op0=ALU.mult,
                                                                op1=ALU.add)
                        else:
                            last = residual(i, h, pb[:, :])
                        last.then_inc(Hf.acc, 1)
                dve.drain().then_inc(res_done, 1)

    @block.scalar
    def _(act):
        act.dma_start(anc_in[:], a["anc"].rearrange("p (c n) -> p c n", c=2)).then_inc(ld_anc, 16)
        act.dma_start(sel_in[:], a["sel"].rearrange("p (h k) -> p h k", h=8)).then_inc(ld_anc, 16)

        def evacuate_xT(n):
            act.wait_ge(xT_ps, n)
            act.activation(xT[:, 0, :], bank[6][:, :], ACT.Copy)
            act.activation(xT[:, 1, :], bank[7][:, :], ACT.Copy)
            act.drain().then_inc(xT_ready, 1)

        evacuate_xT(1)

        if phases > 0:
            with act.Fori(0, PAIRS) as i:
                for j in range(2):
                    act.wait_ge(A.kv, i * 2 + (j + 1))
                    act.activation(pk[:, j, :], bank[j][0:SK, 0:D], ACT.Silu,
                                   scale=tokm[0:SK, ds(i * 2 + j, 1)]).then_inc(A.pk, 1)
                for j in range(2):
                    act.wait_ge(A.kvo, i * 2 + (j + 1))
                    act.activation(kvoS[:, j, :, :].rearrange("p k n -> p (k n)"), bank[2 + j][:, :],
                                   ACT.Copy).then_inc(A.kvoS, 1)
                evacuate_xT(i + 2)

        if phases > 1:
            with act.Fori(0, PAIRS) as i:
                for p in range(TREES):
                    for c, n in ((0, INNER), (1, LEAVES)):
                        act.wait_ge(Bf.logits, i * (2 * TREES) + (2 * p + c + 1))
                        if c == 0:
                            act.wait_ge(Bf.dec, i * TREES + (p + 1))
                        if p >= 2:
                            act.wait_ge(Bf.msk, i * (2 * TREES) + (2 * p - 2))
                        act.activation(act0[0:n, p % 2, c, :], bank[2 + 2 * (p % 2) + c][0:n, :], ACT.Silu,
                                       bias=bin2[0:n, p, c:c + 1]).then_inc(Bf.act, 1)
                evacuate_xT(i + (4 * 1 + 2))

        def attention(L):
            s, dh, ph = X[L.name], L.dh, L.phase
            if L is not L1X:
                act.wait_ge(bias_done, 1)
            with act.Fori(0, PAIRS) as i:
                act.wait_ge(s.kp, i + 1)
                for g in range(4):
                    ps = bank[2 + g // 2][:, (g % 2) * 2 * SK:(g % 2) * 2 * SK + 2 * SK]
                    if L is L1X:
                        act.activation(k32[:, g, :], ps, ACT.Copy, scale=L.scale)
                    else:
                        c = 6 * (L.order - 2) + 2 + g
                        act.activation(k32[:, g, :], ps, ACT.Identity, bias=bias2[:, c:c + 1], scale=L.scale)
                act.drain().then_inc(s.k32, 1)
                act.wait_ge(s.qp, i + 1)
                for g in range(4):
                    f, src = g // 2, slice(64 * (g % 2), 64 * (g % 2) + 64)
                    if L is L1X:
                        act.activation(Q2[src, g, :], bank[f][src, :], ACT.Copy).then_inc(s.qhi, 1)
                    else:
                        c = 6 * (L.order - 2) + f
                        act.activation(Q2[src, g, :], bank[f][src, :], ACT.Identity,
                                       bias=bias2[src, c:c + 1]).then_inc(s.qhi, 1)
                if L is L1X:
                    act.wait_ge(s.vp, i + 1)
                    act.activation(v32[:].rearrange("p b n -> p (b n)"), bank[4][0:SK, :], ACT.Copy).then_inc(s.v32, 1)
                for t in range(TT):
                    act.wait_ge(s.mt, i * TT + (t + 1))
                    act.activation(MBT[:, 0:L.sets, t * 128:t * 128 + 128],
                                   bankh[6 + t % 2][:, 0:L.sets * 128].rearrange("p (h n) -> p h n", h=L.sets),
                                   ACT.Copy).then_inc(s.mbt, 1)

                def high_part(u):
                    act.wait_ge(s.exp, i * L.units + (u + 1))
                    if u >= 3:
                        act.wait_ge(s.pv, i * L.units + (u - 2))
                    act.activation(phi[:, u % 3, :], e32[:, u % 3, :], ACT.Copy).then_inc(s.phi, 1)

                for u in range(L.units):
                    act.wait_ge(s.sc, i * L.units + (u + 1))
                    if u >= 3:
                        act.wait_ge(s.lo, i * L.units + (u - 2))
                    act.activation(e32[:, u % 3, :], bank[2 + u % 4][0:SK, :], ACT.Exp).then_inc(s.exp, 1)
                    if u >= 1:
                        high_part(u - 1)
                high_part(L.units - 1)
                if L is not L1X:
                    act.wait_ge(s.oT, i + 1)
                    act.activation(oT[:, 0, :], bank[0][:, :], ACT.Copy)
                    act.activation(oT[:, 1, :], bank[1][:, :], ACT.Copy)
                    act.drain().then_inc(s.oTs, 1)
                evacuate_xT(i + (4 * ph + 2))

        if phases > 2:
            attention(L1X)

        if phases > 3:
            with act.Fori(0, PAIRS) as i:
                act.wait_ge(Df.sb, i + 1)
                act.activation(sB[:], bank[5][:, :], ACT.Copy).then_inc(Df.sB, 1)
                act.wait_ge(Df.xqt, i + 1)
                act.activation(xqT[:, 0, :], bankh[6][:, 0:TOK], ACT.Copy)
                act.activation(xqT[:, 1, :], bankh[7][:, 0:TOK], ACT.Copy)
                act.drain().then_inc(Df.xqT, 1)

                def silu(t):
                    act.wait_ge(Df.conv, i * HT + (t + 1))
                    act.activation(ha[:, t, :], yc[:, t % 3, :], ACT.Silu).then_inc(Df.silu, 1)

                for t in range(HT):
                    act.wait_ge(Df.deq, i * HT + (t + 1))
                    if t >= 3:
                        act.wait_ge(Df.silu, i * HT + (t - 2))
                    act.activation(yc[:, t % 3, :].rearrange("p (b s) -> p b s", b=2), hpad[:, t % 2, :, 1:S + 1],
                                   ACT.Identity, bias=cb[:, t:t + 1], scale=cw[:, t, 1:2]).then_inc(Df.mid, 1)
                    if t >= 1:
                        silu(t - 1)
                silu(HT - 1)
                evacuate_xT(i + (4 * 3 + 2))

        if phases > 4:
            attention(L2X)

        if phases > 5:
            with act.Fori(0, PAIRS) as i:
                for t in range(HT):
                    act.wait_ge(Ff.gate, i * HT + (t + 1))
                    if t >= 2:
                        act.wait_ge(Ff.h0, i * HT + (t - 1))
                    act.activation(sg[:, t % 2, :], bank[2 * (t % 2)][:, :], ACT.Silu,
                                   scale=s12[:, 0, t:t + 1]).then_inc(Ff.silu, 1)
                for t in range(HT):
                    act.wait_ge(Ff.p1, i * HT + (t + 1))
                    act.activation(hb[:, t, :], bank[[4, 5, 0, 1][t % 4]][:, :], ACT.Gelu,
                                   scale=s12[:, 2, t:t + 1]).then_inc(Ff.h1, 1)
                evacuate_xT(i + (4 * 5 + 2))
                for t in range(HT):
                    act.wait_ge(Ff.p2, i * HT + (t + 1))
                    act.activation(ha[:, t, :], bank[[2, 3, 0, 1][t % 4]][:, :], ACT.Gelu,
                                   scale=s12[:, 3, t:t + 1]).then_inc(Ff.h2, 1)

        if phases > 6:
            attention(L3X)

        if phases > 7:
            with act.Fori(0, PAIRS) as i:
                act.wait_ge(Hf.gl, i + 1)
                act.activation(gex[:], gl[:], ACT.Exp).then_inc(Hf.gex, 1)
                act.wait_ge(Hf.gt, i + 1)
                act.activation(gT[:], bank[3][0:NE, :], ACT.Copy).then_inc(Hf.gT, 1)
                for e in range(NE):
                    act.wait_ge(Hf.up, i * NE + (e + 1))
                    if e >= 2:
                        act.wait_ge(Hf.eo, i * (2 * NE + 2) + (2 * e - 2))
                    for f in range(K2):
                        act.activation(he[:, e % 2, f, :], bank[(0, 6)[e % 2] + f][:, :], ACT.Gelu,
                                       bias=b1e[:, e, f:f + 1])
                    act.drain().then_inc(Hf.he, 1)
                evacuate_xT(i + (4 * 7 + 2))

    @block.tensor
    def _(pe):
        def transpose_rows(n):
            pe.wait_ge(xln_ready, n)
            for k in range(K2):
                for t in range(TT):
                    last = pe.transpose(bank[6 + k][:, t * 128:t * 128 + 128], xln[:, t, k * 128:k * 128 + 128],
                                        ident[:])
            last.then_inc(xT_ps, 1)

        def tok(t):
            return slice(t * 128, t * 128 + 128)

        pe.wait_ge(ld_const, LD_CONST)
        pe.wait_ge(filled, 1)
        transpose_rows(1)
        pe.wait_ge(ld_l0, LD_L0)
        for f in range(K2):
            for k in range(K2):
                last = pe.matmul(bank[0][:, f * D:f * D + D], stage_wvT[:, k, f * 128:f * 128 + 128], stage_wo[:, k, :],
                                 start=(k == 0), stop=(k == K2 - 1))
        last.then_inc(wvo_ps, 1)
        pe.wait_ge(wvo_done, 1)

        if phases > 0:
            with pe.Fori(0, PAIRS) as i:
                pe.wait_ge(res_done, i + 1)
                pe.wait_ge(ctx_ready, i * 16 + 16)
                for j in range(2):
                    for k in range(K2):
                        last = pe.matmul(bank[j][0:SK, :], ctxp[:, k, j * SK:j * SK + SK], wkvo[:, k, :],
                                         start=(k == 0), stop=(k == K2 - 1))
                    last.then_inc(A.kv, 1)
                for j in range(2):
                    pe.wait_ge(A.pk, i * 2 + (j + 1))
                    pe.wait_ge(A.pvo, i * 2 + (j + 1))
                    for f in range(K2):
                        last = pe.matmul(bank[2 + j][:, f * D:f * D + D], pk[:, j, f * 128:f * 128 + 128], pvo[:, j, :],
                                         start=True, stop=True)
                    last.then_inc(A.kvo, 1)
                for j in range(2):
                    pe.wait_ge(A.kvoS, i * 2 + (j + 1))
                    for f in range(K2):
                        for k in range(K2):
                            last = pe.matmul(bank[j][:, f * D:f * D + D], wqT0[:, k, f * 128:f * 128 + 128],
                                             kvoS[:, j, k, :], start=(k == 0), stop=(k == K2 - 1))
                    last.then_inc(A.g, 1)
                pe.wait_ge(xT_ready, i + 1)
                for j in range(2):
                    pe.wait_ge(A.gS, i * 2 + (j + 1))
                    for q in range(2):
                        for k in range(K2):
                            last = pe.matmul(bank[4 + j][:, q * D:q * D + D], xT[:, k, tok(2 * j + q)],
                                             gS[:, j, k, :], start=(k == 0), stop=(k == K2 - 1))
                    last.then_inc(A.out, 1)
                transpose_rows(i + 2)

        if phases > 1:
            pe.wait_ge(consts, 1)
            pe.wait_ge(ld_in, LD_IN)
            pe.wait_ge(ld_out_w, LD_OUT)
            with pe.Fori(0, PAIRS) as i:
                pe.wait_ge(res_done, i + (4 + 1))
                pe.wait_ge(xT_ready, i + (4 + 1))
                for step in range(TREES + 2):
                    p = step
                    if p < TREES:
                        if p >= 2:
                            pe.wait_ge(Bf.act, i * (2 * TREES) + (2 * p - 2))
                        for c, n in ((0, INNER), (1, LEAVES)):
                            w0 = NODES * p + INNER * c
                            for k in range(K2):
                                last = pe.matmul(bank[2 + 2 * (p % 2) + c][0:n, :], winT[:, k, w0:w0 + n], xT[:, k, :],
                                                 start=(k == 0), stop=(k == K2 - 1))
                            last.then_inc(Bf.logits, 1)
                    p = step - 1
                    if 0 <= p < TREES:
                        pe.wait_ge(Bf.dec, i * TREES + (p + 1))
                        if p >= 1:
                            pe.wait_ge(Bf.msk, i * (2 * TREES) + 2 * p)
                        for c, n in ((0, INNER), (1, LEAVES)):
                            last = pe.matmul(bank[6 + c][0:n, :], anc[0:INNER, c, 0:n], dec0[0:INNER, p % 2, :],
                                             start=True, stop=True)
                        last.then_inc(Bf.cnt, 1)
                    p = step - 2
                    if 0 <= p < TREES:
                        for c, n in ((0, INNER), (1, LEAVES)):
                            pe.wait_ge(Bf.msk, i * (2 * TREES) + (2 * p + c + 1))
                            for t in range(TT):
                                last = pe.matmul(bank[t // 2][:, (t % 2) * D:(t % 2) * D + D],
                                                 msk0[0:n, p % 2, c, tok(t)], woutT[0:n, 2 * p + c, :],
                                                 start=(p == 0 and c == 0 and t % 2 == 0),
                                                 stop=(p == TREES - 1 and c == 1), skip_group_check=True)
                last.then_inc(Bf.out, 1)
                transpose_rows(i + (4 + 2))

        def attention(L):
            s, HG, dh, ph, w = X[L.name], L.hg, L.dh, L.phase, proj[L.name]
            n_units, n_ap = L.units, L.approx
            with pe.Fori(0, PAIRS) as i:
                pe.wait_ge(res_done, i + (4 * ph + 1))
                pe.wait_ge(ctx_ready, i * 16 + 16 * (4 * L.order + 1))
                for g in range(4):
                    f = g // 2
                    for k in ((f,) if L is L1X else range(K2)):
                        lhs = bdk[:, g % 2, :] if L is L1X else w[1][:, k, g * 128:g * 128 + 128]
                        last = pe.matmul(bank[2 + g // 2][:, (g % 2) * 2 * SK:(g % 2) * 2 * SK + 2 * SK], lhs,
                                         ctxp[:, k, :], start=(L is L1X or k == 0), stop=(L is L1X or k == K2 - 1))
                last.then_inc(s.kp, 1)
                for b in range(2):
                    for f in range(K2):
                        if L is L1X:
                            last = pe.matmul(bank[4][0:SK, b * D + f * 128:b * D + f * 128 + 128],
                                             ctxp[:, f, b * SK:b * SK + SK], bdv[:], start=True, stop=True)
                        else:
                            last = pe.matmul(bank[4][0:SK, b * D:b * D + D], ctxp[:, f, b * SK:b * SK + SK],
                                             w[2][:, f, :], start=(f == 0), stop=(f == K2 - 1))
                last.then_inc(s.vp, 1)
                pe.wait_ge(xT_ready, i + (4 * ph + 1))
                for f in range(K2):
                    for k in ((f,) if L is L1X else range(K2)):
                        lhs = bdq[:] if L is L1X else w[0][:, k, f * 128:f * 128 + 128]
                        last = pe.matmul(bank[f][:, :], lhs, xT[:, k, :], start=(L is L1X or k == 0),
                                         stop=(L is L1X or k == K2 - 1))
                last.then_inc(s.qp, 1)
                pe.wait_ge(s.kpad, i + 1)
                pe.wait_ge(s.qlo, i + 1)
                pe.wait_ge(s.v2, i + 1)
                pe.wait_ge(s.mb, i + 1)

                def transpose_maxima(t):
                    pe.wait_ge(s.red, i * n_ap + (t + 1) * (L.heads // 4))
                    if t >= 2:
                        pe.wait_ge(s.mbt, i * TT + (t - 1))
                    for h in range(L.sets):
                        last = pe.transpose(bankh[6 + t % 2][:, h * 128:h * 128 + 128], MB[:, t, h, :], identb[:])
                    last.then_inc(s.mt, 1)

                for t in range(TT):
                    for q in range(L.heads // 4):
                        n = t * (L.heads // 4) + q
                        if n >= 4:
                            pe.wait_ge(s.red, i * n_ap + (n - 3))
                        g, r0, b = 4 * q // HG, 4 * q % HG, t // 2
                        ps = bank[2 + n % 4][:, 0:4 * SK]
                        pe.matmul(ps, Q2[:, g, tok(t)], Kpad[:, 0, r0:r0 + 4, g, b * SK:b * SK + SK],
                                  start=True, stop=False)
                        pe.matmul(ps, identb[:], MB[:, t, 0, 0:SK].unsqueeze(1).broadcast_to([128, 4, SK]),
                                  start=False, stop=True).then_inc(s.ap, 1)
                    if t >= 1:
                        transpose_maxima(t - 1)
                transpose_maxima(TT - 1)
                pe.wait_ge(s.mbt, i * TT + TT)

                def scores(u):
                    if u >= 4:
                        pe.wait_ge(s.exp, i * n_units + (u - 3))
                    b = u // (n_units // 2)
                    qs = slice(b * S, b * S + S)
                    for q in range(2):
                        h = 2 * (u % (n_units // 2)) + q
                        g, r = h // HG, h % HG
                        ps = bank[2 + u % 4][0:SK, q * S:q * S + S]
                        for v in range(2):
                            pe.matmul(ps, Kpad[:, v, r, g, b * SK:b * SK + SK], Q2[:, g, qs], start=(v == 0),
                                      stop=False)
                        pe.matmul(ps, selm[:], MBT[:, h // 8, qs], start=False, stop=False)
                        last = pe.matmul(ps, sels[:, h % 8, :], MBT[:, h // 8, qs], start=False, stop=True)
                    last.then_inc(s.sc, 1)

                def values(u):
                    b = u // (n_units // 2)
                    st = u // (n_units // 4)
                    if st >= 2 and u % (n_units // 4) == 0:
                        pe.wait_ge(s.pvc, i * 4 + (st - 1))
                    pe.wait_ge(s.lo, i * n_units + (u + 1))
                    for q in range(2):
                        h = 2 * (u % (n_units // 2)) + q
                        c0 = (h % L.pvh) * 2 * (dh + 1)
                        rhs = v2(L, b)[:, h, :, :].rearrange("p v d -> p (v d)")
                        for t in range(2):
                            ps = bank[(0, 6)[st % 2] + t][:, c0:c0 + 2 * (dh + 1)]
                            cols = slice(q * S + t * 128, q * S + t * 128 + 128)
                            pe.matmul(ps, phi[:, u % 3, cols], rhs, start=True, stop=False)
                            last = pe.matmul(ps, plo[:, u % 3, cols], rhs, start=False, stop=True)
                    last.then_inc(s.pv, 1)

                for u in range(n_units):
                    scores(u)
                    if u >= 2:
                        values(u - 2)
                values(n_units - 2)
                values(n_units - 1)
                if L is L1X:
                    pe.wait_ge(s.pvc, i * 4 + 4)
                else:
                    pe.wait_ge(s.o, i + 1)
                    for k in range(K2):
                        for t in range(TT):
                            last = pe.transpose(bank[k][:, tok(t)], o[:, t, k * 128:k * 128 + 128], ident[:])
                    last.then_inc(s.oT, 1)
                    pe.wait_ge(s.oTs, i + 1)
                    for t in range(TT):
                        for k in range(K2):
                            last = pe.matmul(bank[2 + t // 2][:, (t % 2) * D:(t % 2) * D + D], oT[:, k, tok(t)],
                                             w[3][:, k, :], start=(k == 0), stop=(k == K2 - 1))
                    last.then_inc(s.out, 1)
                transpose_rows(i + (4 * ph + 2))

        if phases > 2:
            pe.wait_ge(wsum, 1)
            pe.wait_ge(res_done, 4 * 2 + 1)
            pe.matmul(bank[1][:, 0:2], ones[:], stage_sum[:], start=True, stop=True).then_inc(wsum_ps, 1)
            pe.wait_ge(wrcp, 1)
            attention(L1X)

        if phases > 3:
            with pe.Fori(0, PAIRS) as i:
                pe.wait_ge(res_done, i + (4 * 3 + 1))
                pe.wait_ge(xT_ready, i + (4 * 3 + 1))
                pe.wait_ge(Df.xq, i + 1)
                pe.matmul(bank[5][:, :], ones[:], dg[:].rearrange("p t n -> p (t n)"), start=True,
                          stop=True).then_inc(Df.sb, 1)
                for k in range(K2):
                    for t in range(TT):
                        last = pe.transpose(bankh[6 + k][:, tok(t)], xq[:, t, k * 128:k * 128 + 128], identb[:])
                last.then_inc(Df.xqt, 1)
                pe.wait_ge(Df.xqT, i + 1)
                for t in range(HT):
                    if t >= 4:
                        pe.wait_ge(Df.deq, i * HT + (t - 3))
                    for k in range(K2):
                        last = pe.matmul(bank[t % 4][:, :], w1q[:, k, tok(t)], xqT[:, k, :], start=(k == 0),
                                         stop=(k == K2 - 1))
                    last.then_inc(Df.up, 1)
                transpose_rows(i + (4 * 3 + 2))
                pe.wait_ge(Df.mrun, i + 1)
                for t in range(TT):
                    last = pe.transpose(bank[4][:, tok(t)], mrun[:, tok(t)], ident[:])
                last.then_inc(Df.mt, 1)
                pe.wait_ge(Df.dgh, i + 1)
                pe.wait_ge(Df.sB, i + 1)
                pe.matmul(bank[5][:, :], ones[:], dg[:].rearrange("p t n -> p (t n)"), start=True,
                          stop=True).then_inc(Df.qb, 1)
                for t in range(TT):
                    for k in range(HT):
                        if t == 0:
                            pe.wait_ge(Df.hq, i * HT + (k + 1))
                        last = pe.matmul(bank[t // 2][:, (t % 2) * D:(t % 2) * D + D], hq[:, k, tok(t)], w2q[:, k, :],
                                         start=(k == 0), stop=(k == HT - 1))
                last.then_inc(Df.out, 1)

        if phases > 4:
            pe.wait_ge(ld_l2, LD_L2)
            attention(L2X)

        if phases > 5:
            pe.wait_ge(ld_h, LD_H)
            with pe.Fori(0, PAIRS) as i:
                pe.wait_ge(res_done, i + (4 * 5 + 1))
                pe.wait_ge(xT_ready, i + (4 * 5 + 1))
                for t in range(HT):
                    if t >= 2:
                        pe.wait_ge(Ff.h0, i * HT + (t - 1))
                    for n, wt in enumerate((f1, f2)):
                        for k in range(K2):
                            last = pe.matmul(bank[2 * (t % 2) + n][:, :], wt[:, k, tok(t)], xT[:, k, :],
                                             start=(k == 0), stop=(k == K2 - 1))
                    last.then_inc(Ff.gate, 1)
                for t in range(HT):
                    if t >= 4:
                        pe.wait_ge(Ff.h1, i * HT + (t - 3))
                    for k in range(HT):
                        if t == 0:
                            pe.wait_ge(Ff.h0, i * HT + (k + 1))
                        last = pe.matmul(bank[[4, 5, 0, 1][t % 4]][:, :], h1w[:, k, tok(t)], ha[:, k, :],
                                         start=(k == 0), stop=(k == HT - 1))
                    last.then_inc(Ff.p1, 1)
                transpose_rows(i + (4 * 5 + 2))
                for t in range(HT):
                    if t >= 4:
                        pe.wait_ge(Ff.h2, i * HT + (t - 3))
                    for k in range(HT):
                        if t == 0:
                            pe.wait_ge(Ff.h1, i * HT + (k + 1))
                        last = pe.matmul(bank[[2, 3, 0, 1][t % 4]][:, :], h2w[:, k, tok(t)], hb[:, k, :],
                                         start=(k == 0), stop=(k == HT - 1))
                    last.then_inc(Ff.p2, 1)
                for t in range(TT):
                    for k in range(HT):
                        if t == 0:
                            pe.wait_ge(Ff.h2, i * HT + (k + 1))
                        last = pe.matmul(bank[4 + t // 2][:, (t % 2) * D:(t % 2) * D + D], ha[:, k, tok(t)],
                                         f3[:, k, :], start=(k == 0), stop=(k == HT - 1))
                    if t % 2:
                        last.then_inc(Ff.out, 1)

        if phases > 6:
            pe.wait_ge(ld_l3, LD_L3)
            attention(L3X)

        if phases > 7:
            with pe.Fori(0, PAIRS) as i:
                pe.wait_ge(res_done, i + (4 * 7 + 1))
                pe.wait_ge(xT_ready, i + (4 * 7 + 1))
                for t in range(TT):
                    for k in range(K2):
                        last = pe.matmul(bank[0][:, t * NE:t * NE + NE], xT[:, k, tok(t)], wg[:, k, :],
                                         start=(k == 0), stop=(k == K2 - 1))
                last.then_inc(Hf.lg, 1)
                pe.wait_ge(Hf.gl, i + 1)
                n_eo = 2 * NE + 2

                def up(e):
                    for f in range(K2):
                        for k in range(K2):
                            last = pe.matmul(bank[(0, 6)[e % 2] + f][:, :], w1e[:, e, k, f * 128:f * 128 + 128],
                                             xT[:, k, :], start=(k == 0), stop=(k == K2 - 1))
                    last.then_inc(Hf.up, 1)

                def half_done(n):
                    if n >= 4:
                        pe.wait_ge(Hf.acc, i * n_eo + (n - 3))

                up(0)
                pe.wait_ge(Hf.gw, i + 1)
                for t in range(TT):
                    last = pe.transpose(bank[3][0:NE, tok(t)], gwt[:, t, :], ident[:])
                last.then_inc(Hf.gt, 1)
                for e in range(NE):
                    if e + 1 < NE:
                        up(e + 1)
                    pe.wait_ge(Hf.he, i * NE + (e + 1))
                    for h in range(2):
                        n = 2 * e + h
                        half_done(n)
                        if n == 3:
                            pe.wait_ge(Hf.gT, i + 1)
                        for q in range(2):
                            for k in range(K2):
                                last = pe.matmul(bank[[4, 5, 2, 3][n % 4]][:, q * D:q * D + D],
                                                 he[:, e % 2, k, tok(2 * h + q)], w2e[:, e, k, :],
                                                 start=(k == 0), stop=(k == K2 - 1))
                        last.then_inc(Hf.eo, 1)
                for h in range(2):
                    n = 2 * NE + h
                    half_done(n)
                    for q in range(2):
                        last = pe.matmul(bank[[4, 5, 2, 3][n % 4]][:, q * D:q * D + D], gT[:, tok(2 * h + q)], b2e[:],
                                         start=True, stop=True)
                    last.then_inc(Hf.eo, 1)
                transpose_rows(i + (4 * 7 + 2))

    es.close()


def constants():
    import numpy as np
    anc = np.zeros((128, 2, 128), np.float32)
    tgt = np.zeros((128, 2), np.float32)
    for n in range(NODES):
        c, r = (0, n) if n < INNER else (1, n - INNER)
        node = n
        while node:
            parent = (node - 1) // 2
            right = node == 2 * parent + 2
            anc[parent, c, r] = 1.0 if right else -1.0
            tgt[r, c] += right
            node = parent
    sel = np.zeros((128, 8, SK), np.float32)
    for h in range(8):
        sel[SK + h, h, :] = -1.0
    rm4 = np.zeros((128, 4), np.float32)
    rm8 = np.zeros((128, 8), np.float32)
    for p in range(128):
        rm4[p, p % 64 // 16] = 1.0
        rm8[p, p % 64 // 8] = 1.0
    return {"ident": np.eye(128, dtype=np.float32), "anc": anc.reshape(128, -1), "sel": sel.reshape(128, -1),
            "tgt": tgt, "rm4": rm4, "rm8": rm8,
            "rev": np.broadcast_to(np.arange(NE, 0, -1, dtype=np.float32), (128, NE)).copy()}


def layout(v):
    import numpy as np
    f = {k: np.asarray(v[k]) for k in v}
    c = np.ascontiguousarray
    bqkv, wqkv = f["L3_xattn_bqkv"], f["L3_xattn_Wqkv"]

    def twice(w):
        return np.repeat(w.reshape(w.shape[0], -1, 1, 64), 2, axis=2).reshape(w.shape[0], -1)

    def blocks(w):
        r = np.zeros((128, 128), w.dtype)
        for h in range(8):
            r[16 * h:16 * h + 16, 16 * h:16 * h + 16] = w.T
        return r

    def columns(t):
        return t.reshape(-1, 128).T

    b_in = f["L0_ffn_b_in"].reshape(TREES, NODES)
    bin2 = np.zeros((128, TREES, 2), b_in.dtype)
    bin2[:INNER, :, 0] = b_in[:, :INNER].T
    bin2[:LEAVES, :, 1] = b_in[:, INNER:].T
    bias2 = np.zeros((128, 2, 6), bqkv.dtype)
    for n, (bq, bk) in enumerate(((f["L2_xattn_bq"], f["L2_xattn_bk"]), (bqkv[0:D], bqkv[D:2 * D]))):
        bias2[:, n, 0:2] = columns(bq)
        for h in range(2):
            bias2[64 * h:64 * h + 64, n, 2:6] = bk.reshape(4, 64).T
    r = {
        "x": f["x"].reshape(B * S, D), "ctxT": f["ctx_1024"].reshape(B * SK, D).T,
        "tokm": f["mask_BxS2x1_ff1"].reshape(B, SK).T,
        "mask": f["mask_Bx1xSxS2_ik1"].reshape(B * S, SK),
        "kpm": f["mask_BxS2_bk0"], "attnm": f["mask_SxS2_bk1"],
        "wk0": f["L0_xattn_Wk"], "wqT0": f["L0_xattn_Wq"].T, "wvT0": f["L0_xattn_Wv"].T, "wo0": f["L0_xattn_Wo"],
        "winT": f["L0_ffn_W_in"].T, "bin2": bin2.reshape(128, -1), "woutT": f["L0_ffn_W_out"].T,
        "bdq": blocks(f["L1_xattn_Wq"]), "bdk": twice(blocks(f["L1_xattn_Wk"])), "bdv": blocks(f["L1_xattn_Wv"]),
        "w1T": f["L1_ffn_w1"].T, "w2T": f["L1_ffn_w2"].T,
        "cw": f["L1_ffn_conv_w"].reshape(HT, 128, 3).transpose(1, 0, 2).reshape(128, -1),
        "cb": columns(f["L1_ffn_conv_b"]),
        "wq2": f["L2_xattn_wq"], "wk2": twice(f["L2_xattn_wk"]), "wv2": f["L2_xattn_wv"], "wo2": f["L2_xattn_wo"],
        "bv2": f["L2_xattn_bv"], "bo2": f["L2_xattn_bo"], "bias2": bias2.reshape(128, -1),
        "f1T": f["L2_ffn_w1_w"].T, "f2T": f["L2_ffn_w2_w"].T, "h1T": f["L2_ffn_h1_w"].T,
        "h2T": f["L2_ffn_h2_w"].T, "f3T": f["L2_ffn_w3_w"].T,
        "s12": np.concatenate([columns(f["L2_ffn_" + n]) for n in ("w1_s", "w2_s", "h1_s", "h2_s")], axis=1),
        "w3_s": f["L2_ffn_w3_s"],
        "wq3": wqkv[:, 0:D], "wk3": twice(wqkv[:, D:2 * D]), "wv3": wqkv[:, 2 * D:3 * D], "wo3": f["L3_xattn_Wo"], "bo3": f["L3_xattn_bo"], "bv3": bqkv[2 * D:3 * D],
        "wg": f["L3_ffn_Wg"], "bg": f["L3_ffn_bg"], "w1e": f["L3_ffn_W1"],
        "b1e": f["L3_ffn_b1"].reshape(NE, K2, 128).transpose(2, 0, 1).reshape(128, -1),
        "w2e": f["L3_ffn_W2"], "b2e": f["L3_ffn_b2"],
    }
    r.update(constants())
    return {k: c(t) for k, t in r.items()}


def kernel(**inputs):
    import concourse.bacc as bacc
    from concourse.bass_utils import run_bass_kernel_spmd

    nc = bacc.Bacc("TRN2", target_bir_lowering=False, num_devices=1)
    arrays = layout(inputs)
    args = {k: nc.dram_tensor("in_" + k, t.shape, mybir.dt.from_np(t.dtype), kind="ExternalInput").ap()
            for k, t in arrays.items()}
    out = nc.dram_tensor("out", [B * S, D], F32, kind="ExternalOutput").ap()
    build(nc, args, out)
    r = run_bass_kernel_spmd(nc, [{"in_" + k: t for k, t in arrays.items()}], core_ids=[0])
    return r.results[0]["out"].reshape(B, S, D)
```
